# Optimizing a Trainium2 kernel written in Bass

```python
import numpy as np
import jax
import jax.numpy as jnp

def _softmax(x, axis=-1):
    return jax.nn.softmax(x, axis=axis)

def _gelu(x):
    return jax.nn.gelu(x, approximate=True)

def _silu(x):
    return jax.nn.silu(x)

def _sigmoid(x):
    return jax.nn.sigmoid(x)

def _layernorm(x, axis=-1, eps=1e-05):
    m = jnp.mean(x, axis=axis, keepdims=True)
    v = jnp.var(x, axis=axis, keepdims=True)
    return (x - m) / jnp.sqrt(v + eps)

def _scatter_add(tgt, idx, src, axis=0):
    return tgt.at[idx].add(src)

def _segment_sum(src, seg, n):
    return jax.ops.segment_sum(src, seg, n)
kernel_name = 'mk_prb_d2_jaxref_r8_d7b606'

def setup_inputs(seed: int=0):
    np.random.seed(seed)
    _w = jnp.asarray

    def _L0_attn_setup():
        import jax, jax.numpy as jnp
        import numpy as np
        D_MODEL = 128
        QHEADS = 16
        KVHEADS = 4
        G = QHEADS // KVHEADS
        D_Q = D_MODEL // QHEADS
        D_KV = D_MODEL // QHEADS * KVHEADS
        BATCH, SEQ = (2, 256)

        def _xavier(key, shape):
            fan_out, fan_in = shape
            lim = (6.0 / (fan_in + fan_out)) ** 0.5
            return jax.random.uniform(key, shape, jnp.float32, -lim, lim)
        key = jax.random.key(seed)
        ks = jax.random.split(key, 5)
        x = jax.random.normal(ks[0], (BATCH, SEQ, D_MODEL), jnp.float32)
        wq = _xavier(ks[1], (D_MODEL, D_MODEL))
        bq = jnp.zeros((D_MODEL,), jnp.float32)
        wk = _xavier(ks[2], (D_KV, D_MODEL))
        bk = jnp.zeros((D_KV,), jnp.float32)
        wv = _xavier(ks[3], (D_KV, D_MODEL))
        bv = jnp.zeros((D_KV,), jnp.float32)
        wo = _xavier(ks[4], (D_MODEL, D_MODEL))
        bo = jnp.zeros((D_MODEL,), jnp.float32)
        return {'x': x, 'wq': wq, 'bq': bq, 'wk': wk, 'bk': bk, 'wv': wv, 'bv': bv, 'wo': wo, 'bo': bo}
    _L0_attn_in = _L0_attn_setup()

    def _L0_ffn_setup():
        import jax, jax.numpy as jnp
        import numpy as np
        D_MODEL = 128
        N_HEADS = 16
        HEAD_DIM = D_MODEL // N_HEADS
        KV_LATENT = 64
        N_EXPERTS = 4
        D_HIDDEN = 4 * D_MODEL
        B, T = (2, 128)

        def rmsnorm(x, w, eps=1e-06):
            return w * (x * jax.lax.rsqrt(jnp.mean(x * x, axis=-1, keepdims=True) + eps))

        def layernorm(x, g, b, eps=1e-05):
            mu = jnp.mean(x, axis=-1, keepdims=True)
            var = jnp.mean((x - mu) ** 2, axis=-1, keepdims=True)
            return (x - mu) * jax.lax.rsqrt(var + eps) * g + b

        def apply_rope(x):
            t, d = (x.shape[2], x.shape[3])
            half = d // 2
            pos = jnp.arange(t, dtype=x.dtype)[:, None]
            inv_freq = 1.0 / 10000.0 ** (jnp.arange(half, dtype=x.dtype) / half)
            ang = pos * inv_freq[None, :]
            sin, cos = (jnp.sin(ang), jnp.cos(ang))
            x1, x2 = (x[..., :half], x[..., half:])
            return jnp.concatenate([x1 * cos - x2 * sin, x1 * sin + x2 * cos], axis=-1)

        def mla_attention(x, Wq, Wdkv, Wuk, Wuv, Wo, ln_g, ln_b):
            b, t, _ = x.shape
            q = (x @ Wq.T).reshape(b, t, N_HEADS, HEAD_DIM).transpose(0, 2, 1, 3)
            latent = layernorm(x @ Wdkv.T, ln_g, ln_b)
            k = (latent @ Wuk.T).reshape(b, t, N_HEADS, HEAD_DIM).transpose(0, 2, 1, 3)
            v = (latent @ Wuv.T).reshape(b, t, N_HEADS, HEAD_DIM).transpose(0, 2, 1, 3)
            q = apply_rope(q)
            k = apply_rope(k)
            scores = jnp.einsum('bhqd,bhkd->bhqk', q, k) / np.sqrt(HEAD_DIM)
            causal = jnp.tril(jnp.ones((t, t), dtype=bool))
            scores = jnp.where(causal, scores, -jnp.inf)
            attn = jax.nn.softmax(scores, axis=-1)
            out = jnp.einsum('bhqk,bhkd->bhqd', attn, v).transpose(0, 2, 1, 3).reshape(b, t, D_MODEL)
            return out @ Wo.T

        def moe(x, gate_w, gate_b, W1, b1, W2, b2):
            logits = x @ gate_w.T + gate_b
            top = jnp.argmax(logits, axis=-1)
            onehot = jax.nn.one_hot(top, N_EXPERTS, dtype=x.dtype)
            h = jax.nn.relu(jnp.einsum('btd,ehd->bteh', x, W1) + b1)
            y = jnp.einsum('bteh,edh->bted', h, W2) + b2
            return jnp.einsum('bted,bte->btd', y, onehot)
        key = jax.random.key(seed)
        ks = jax.random.split(key, 16)
        s = lambda fan_in: 1.0 / np.sqrt(fan_in)
        return {'x': jax.random.normal(ks[0], (B, T, D_MODEL), jnp.float32), 'norm1_w': jnp.ones((D_MODEL,), jnp.float32), 'norm2_w': jnp.ones((D_MODEL,), jnp.float32), 'Wq': jax.random.normal(ks[1], (D_MODEL, D_MODEL), jnp.float32) * s(D_MODEL), 'Wdkv': jax.random.normal(ks[2], (KV_LATENT, D_MODEL), jnp.float32) * s(D_MODEL), 'Wuk': jax.random.normal(ks[3], (D_MODEL, KV_LATENT), jnp.float32) * s(KV_LATENT), 'Wuv': jax.random.normal(ks[4], (D_MODEL, KV_LATENT), jnp.float32) * s(KV_LATENT), 'Wo': jax.random.normal(ks[5], (D_MODEL, D_MODEL), jnp.float32) * s(D_MODEL), 'ln_g': jnp.ones((KV_LATENT,), jnp.float32), 'ln_b': jnp.zeros((KV_LATENT,), jnp.float32), 'gate_w': jax.random.normal(ks[6], (N_EXPERTS, D_MODEL), jnp.float32) * s(D_MODEL), 'gate_b': jnp.zeros((N_EXPERTS,), jnp.float32), 'W1': jax.random.normal(ks[7], (N_EXPERTS, D_HIDDEN, D_MODEL), jnp.float32) * s(D_MODEL), 'b1': jnp.zeros((N_EXPERTS, D_HIDDEN), jnp.float32), 'W2': jax.random.normal(ks[8], (N_EXPERTS, D_MODEL, D_HIDDEN), jnp.float32) * s(D_HIDDEN), 'b2': jnp.zeros((N_EXPERTS, D_MODEL), jnp.float32)}
    _L0_ffn_in = _L0_ffn_setup()

    def _L1_attn_setup():
        import jax, jax.numpy as jnp
        import numpy as np
        HIDDEN = 128
        HEADS = 16
        HEAD_DIM = HIDDEN // HEADS
        B, S = (4, 256)
        key = jax.random.key(seed)
        ks = jax.random.split(key, 9)
        sd = 1.0 / np.sqrt(HIDDEN)
        return {'hidden_state': jax.random.normal(ks[0], (B, S, HIDDEN), dtype=jnp.float32), 'Wq': jax.random.uniform(ks[1], (HIDDEN, HIDDEN), jnp.float32, -sd, sd), 'bq': jax.random.uniform(ks[2], (HIDDEN,), jnp.float32, -sd, sd), 'Wk': jax.random.uniform(ks[3], (HIDDEN, HEAD_DIM), jnp.float32, -sd, sd), 'bk': jax.random.uniform(ks[4], (HEAD_DIM,), jnp.float32, -sd, sd), 'Wv': jax.random.uniform(ks[5], (HIDDEN, HEAD_DIM), jnp.float32, -sd, sd), 'bv': jax.random.uniform(ks[6], (HEAD_DIM,), jnp.float32, -sd, sd), 'Wo': jax.random.uniform(ks[7], (HIDDEN, HIDDEN), jnp.float32, -sd, sd), 'bo': jax.random.uniform(ks[8], (HIDDEN,), jnp.float32, -sd, sd)}
    _L1_attn_in = _L1_attn_setup()

    def _L1_ffn_setup():
        import jax, jax.numpy as jnp
        import numpy as np
        DIM = 128
        HIDDEN = 384
        SCALE = 1.0 / 127.0

        def _dequant(w_int, dtype):
            return w_int.astype(dtype) * jnp.asarray(SCALE, dtype)
        key = jax.random.key(seed)
        k_x, k_g, k_u, k_d = jax.random.split(key, 4)
        x = jax.random.normal(k_x, (4, 256, DIM), dtype=jnp.float32)
        w_gate = jax.random.randint(k_g, (HIDDEN, DIM), -127, 128, dtype=jnp.int32)
        w_up = jax.random.randint(k_u, (HIDDEN, DIM), -127, 128, dtype=jnp.int32)
        w_down = jax.random.randint(k_d, (DIM, HIDDEN), -127, 128, dtype=jnp.int32)
        return {'x': x, 'w_gate': w_gate, 'w_up': w_up, 'w_down': w_down}
    _L1_ffn_in = _L1_ffn_setup()
    _d = {'L0_attn_x': _L0_attn_in['x'], 'L0_attn_wq': _L0_attn_in['wq'], 'L0_attn_bq': _L0_attn_in['bq'], 'L0_attn_wk': _L0_attn_in['wk'], 'L0_attn_bk': _L0_attn_in['bk'], 'L0_attn_wv': _L0_attn_in['wv'], 'L0_attn_bv': _L0_attn_in['bv'], 'L0_attn_wo': _L0_attn_in['wo'], 'L0_attn_bo': _L0_attn_in['bo'], 'L0_ffn_norm1_w': _L0_ffn_in['norm1_w'], 'L0_ffn_norm2_w': _L0_ffn_in['norm2_w'], 'L0_ffn_Wq': _L0_ffn_in['Wq'], 'L0_ffn_Wdkv': _L0_ffn_in['Wdkv'], 'L0_ffn_Wuk': _L0_ffn_in['Wuk'], 'L0_ffn_Wuv': _L0_ffn_in['Wuv'], 'L0_ffn_Wo': _L0_ffn_in['Wo'], 'L0_ffn_ln_g': _L0_ffn_in['ln_g'], 'L0_ffn_ln_b': _L0_ffn_in['ln_b'], 'L0_ffn_gate_w': _L0_ffn_in['gate_w'], 'L0_ffn_gate_b': _L0_ffn_in['gate_b'], 'L0_ffn_W1': _L0_ffn_in['W1'], 'L0_ffn_b1': _L0_ffn_in['b1'], 'L0_ffn_W2': _L0_ffn_in['W2'], 'L0_ffn_b2': _L0_ffn_in['b2'], 'L1_attn_Wq': _L1_attn_in['Wq'], 'L1_attn_bq': _L1_attn_in['bq'], 'L1_attn_Wk': _L1_attn_in['Wk'], 'L1_attn_bk': _L1_attn_in['bk'], 'L1_attn_Wv': _L1_attn_in['Wv'], 'L1_attn_bv': _L1_attn_in['bv'], 'L1_attn_Wo': _L1_attn_in['Wo'], 'L1_attn_bo': _L1_attn_in['bo'], 'L1_ffn_w_gate': _L1_ffn_in['w_gate'], 'L1_ffn_w_up': _L1_ffn_in['w_up'], 'L1_ffn_w_down': _L1_ffn_in['w_down']}
    _x0 = _d['L0_attn_x']
    _d['L0_attn_x'] = jax.random.normal(jax.random.fold_in(jax.random.key(seed), 1), (16, 512, 128), dtype=_x0.dtype)
    del _x0
    return _d

def reference(L0_attn_x, L0_attn_wq, L0_attn_bq, L0_attn_wk, L0_attn_bk, L0_attn_wv, L0_attn_bv, L0_attn_wo, L0_attn_bo, L0_ffn_norm1_w, L0_ffn_norm2_w, L0_ffn_Wq, L0_ffn_Wdkv, L0_ffn_Wuk, L0_ffn_Wuv, L0_ffn_Wo, L0_ffn_ln_g, L0_ffn_ln_b, L0_ffn_gate_w, L0_ffn_gate_b, L0_ffn_W1, L0_ffn_b1, L0_ffn_W2, L0_ffn_b2, L1_attn_Wq, L1_attn_bq, L1_attn_Wk, L1_attn_bk, L1_attn_Wv, L1_attn_bv, L1_attn_Wo, L1_attn_bo, L1_ffn_w_gate, L1_ffn_w_up, L1_ffn_w_down):

    def _L0_attn_ref(x, wq, bq, wk, bk, wv, bv, wo, bo):
        import jax, jax.numpy as jnp
        import numpy as np
        D_MODEL = 128
        QHEADS = 16
        KVHEADS = 4
        G = QHEADS // KVHEADS
        D_Q = D_MODEL // QHEADS
        D_KV = D_MODEL // QHEADS * KVHEADS
        BATCH, SEQ = (2, 256)

        def _xavier(key, shape):
            fan_out, fan_in = shape
            lim = (6.0 / (fan_in + fan_out)) ** 0.5
            return jax.random.uniform(key, shape, jnp.float32, -lim, lim)
        b, n, _ = x.shape
        scaling = D_Q ** (-0.5)
        q = (x @ wq.T + bq).reshape(b, n, QHEADS, D_Q).transpose(0, 2, 1, 3)
        k = (x @ wk.T + bk).reshape(b, n, KVHEADS, D_Q).transpose(0, 2, 1, 3)
        v = (x @ wv.T + bv).reshape(b, n, KVHEADS, D_Q).transpose(0, 2, 1, 3)
        q = q.reshape(b, KVHEADS, G, n, D_Q).transpose(0, 2, 1, 3, 4)
        attn = jnp.einsum('bghnd,bhsd->bghns', q, k) * scaling
        attn = jax.nn.softmax(attn, axis=-1)
        out = jnp.einsum('bghns,bhsd->bghnd', attn, v)
        out = out.transpose(0, 3, 2, 1, 4).reshape(b, n, D_MODEL)
        return out @ wo.T + bo

    def _L0_ffn_ref(x, norm1_w, norm2_w, Wq, Wdkv, Wuk, Wuv, Wo, ln_g, ln_b, gate_w, gate_b, W1, b1, W2, b2):
        import jax, jax.numpy as jnp
        import numpy as np
        D_MODEL = 128
        N_HEADS = 16
        HEAD_DIM = D_MODEL // N_HEADS
        KV_LATENT = 64
        N_EXPERTS = 4
        D_HIDDEN = 4 * D_MODEL
        B, T = (2, 128)

        def rmsnorm(x, w, eps=1e-06):
            return w * (x * jax.lax.rsqrt(jnp.mean(x * x, axis=-1, keepdims=True) + eps))

        def layernorm(x, g, b, eps=1e-05):
            mu = jnp.mean(x, axis=-1, keepdims=True)
            var = jnp.mean((x - mu) ** 2, axis=-1, keepdims=True)
            return (x - mu) * jax.lax.rsqrt(var + eps) * g + b

        def apply_rope(x):
            t, d = (x.shape[2], x.shape[3])
            half = d // 2
            pos = jnp.arange(t, dtype=x.dtype)[:, None]
            inv_freq = 1.0 / 10000.0 ** (jnp.arange(half, dtype=x.dtype) / half)
            ang = pos * inv_freq[None, :]
            sin, cos = (jnp.sin(ang), jnp.cos(ang))
            x1, x2 = (x[..., :half], x[..., half:])
            return jnp.concatenate([x1 * cos - x2 * sin, x1 * sin + x2 * cos], axis=-1)

        def mla_attention(x, Wq, Wdkv, Wuk, Wuv, Wo, ln_g, ln_b):
            b, t, _ = x.shape
            q = (x @ Wq.T).reshape(b, t, N_HEADS, HEAD_DIM).transpose(0, 2, 1, 3)
            latent = layernorm(x @ Wdkv.T, ln_g, ln_b)
            k = (latent @ Wuk.T).reshape(b, t, N_HEADS, HEAD_DIM).transpose(0, 2, 1, 3)
            v = (latent @ Wuv.T).reshape(b, t, N_HEADS, HEAD_DIM).transpose(0, 2, 1, 3)
            q = apply_rope(q)
            k = apply_rope(k)
            scores = jnp.einsum('bhqd,bhkd->bhqk', q, k) / np.sqrt(HEAD_DIM)
            causal = jnp.tril(jnp.ones((t, t), dtype=bool))
            scores = jnp.where(causal, scores, -jnp.inf)
            attn = jax.nn.softmax(scores, axis=-1)
            out = jnp.einsum('bhqk,bhkd->bhqd', attn, v).transpose(0, 2, 1, 3).reshape(b, t, D_MODEL)
            return out @ Wo.T

        def moe(x, gate_w, gate_b, W1, b1, W2, b2):
            logits = x @ gate_w.T + gate_b
            top = jnp.argmax(logits, axis=-1)
            onehot = jax.nn.one_hot(top, N_EXPERTS, dtype=x.dtype)
            h = jax.nn.relu(jnp.einsum('btd,ehd->bteh', x, W1) + b1)
            y = jnp.einsum('bteh,edh->bted', h, W2) + b2
            return jnp.einsum('bted,bte->btd', y, onehot)
        x = x + mla_attention(rmsnorm(x, norm1_w), Wq, Wdkv, Wuk, Wuv, Wo, ln_g, ln_b)
        x = x + moe(rmsnorm(x, norm2_w), gate_w, gate_b, W1, b1, W2, b2)
        return x

    def _L1_attn_ref(hidden_state, Wq, bq, Wk, bk, Wv, bv, Wo, bo):
        import jax, jax.numpy as jnp
        import numpy as np
        HIDDEN = 128
        HEADS = 16
        HEAD_DIM = HIDDEN // HEADS
        B, S = (4, 256)
        b, s, _ = hidden_state.shape
        q = hidden_state @ Wq + bq
        k = hidden_state @ Wk + bk
        v = hidden_state @ Wv + bv
        q = q.reshape(b, s, HEADS, HEAD_DIM)
        scale = 1.0 / jnp.sqrt(jnp.float32(HEAD_DIM))
        scores = jnp.einsum('bqhd,bkd->bhqk', q, k) * scale
        probs = jax.nn.softmax(scores, axis=-1)
        out = jnp.einsum('bhqk,bkd->bqhd', probs, v)
        out = out.reshape(b, s, HEADS * HEAD_DIM)
        return out @ Wo + bo

    def _L1_ffn_ref(x, w_gate, w_up, w_down):
        import jax, jax.numpy as jnp
        import numpy as np
        DIM = 128
        HIDDEN = 384
        SCALE = 1.0 / 127.0

        def _dequant(w_int, dtype):
            return w_int.astype(dtype) * jnp.asarray(SCALE, dtype)
        wg = _dequant(w_gate, x.dtype)
        wu = _dequant(w_up, x.dtype)
        wd = _dequant(w_down, x.dtype)
        gate = jnp.einsum('bsd,hd->bsh', x, wg)
        up = jnp.einsum('bsd,hd->bsh', x, wu)
        h = jax.nn.silu(gate) * up
        return jnp.einsum('bsh,dh->bsd', h, wd)
    x = L0_attn_x
    xn = _layernorm(x, axis=-1)
    x = x + _L0_attn_ref(xn, L0_attn_wq, L0_attn_bq, L0_attn_wk, L0_attn_bk, L0_attn_wv, L0_attn_bv, L0_attn_wo, L0_attn_bo) + _L0_ffn_ref(xn, L0_ffn_norm1_w, L0_ffn_norm2_w, L0_ffn_Wq, L0_ffn_Wdkv, L0_ffn_Wuk, L0_ffn_Wuv, L0_ffn_Wo, L0_ffn_ln_g, L0_ffn_ln_b, L0_ffn_gate_w, L0_ffn_gate_b, L0_ffn_W1, L0_ffn_b1, L0_ffn_W2, L0_ffn_b2)
    xn = _layernorm(x, axis=-1)
    x = x + _L1_attn_ref(xn, L1_attn_Wq, L1_attn_bq, L1_attn_Wk, L1_attn_bk, L1_attn_Wv, L1_attn_bv, L1_attn_Wo, L1_attn_bo) + _L1_ffn_ref(xn, L1_ffn_w_gate, L1_ffn_w_up, L1_ffn_w_down)
    return x

_drawn_inputs = setup_inputs


def setup_inputs(seed=0):
    import zlib

    import numpy as np

    out = dict(_drawn_inputs(seed))
    spreads = {'L0_attn_bq': (0.0, 0.651),
     'L0_attn_bk': (0.0, 2.0),
     'L0_attn_bv': (0.0, 0.1),
     'L0_attn_bo': (0.0, 0.1),
     'L0_ffn_norm1_w': (1.0, 0.2),
     'L0_ffn_norm2_w': (1.0, 0.2),
     'L0_ffn_ln_g': (1.0, 0.2),
     'L0_ffn_ln_b': (0.0, 0.1),
     'L0_ffn_gate_b': (0.0, 0.1),
     'L0_ffn_b1': (0.0, 0.1),
     'L0_ffn_b2': (0.0, 0.1)}
    factors = {'L1_attn_Wq': 8.0,
     'L1_attn_bq': 23.719,
     'L1_attn_Wk': 8.0,
     'L1_attn_bk': 200.0,
     'L1_attn_Wv': 8.0,
     'L1_attn_bv': 64.0,
     'L1_attn_Wo': 8.0,
     'L1_attn_bo': 200.0}
    for name, (base, spread) in spreads.items():
        noise = np.random.default_rng([zlib.crc32(name.encode()), seed]).standard_normal(out[name].shape)
        drawn = base * np.exp(spread * noise) if base else spread * noise
        out[name] = jnp.asarray(drawn.astype(out[name].dtype))
    for name, factor in factors.items():
        out[name] = (out[name] * factor).astype(out[name].dtype)
    return out
```

```python
from contextlib import ExitStack

import numpy as np
import concourse.bass as bass
from concourse import mybir

F32 = mybir.dt.float32
BF16 = mybir.dt.bfloat16
I32 = mybir.dt.int32
ALU = mybir.AluOpType
ACT = mybir.ActivationFunctionType
AX = mybir.AxisListType

P = 128
BATCH, SEQ, D = 16, 512, 128
TILES = SEQ // P
HEADS, HD = 16, 8
GROUP = 4
GROUPS = HEADS // GROUP
VW = 32
KV0 = 4
LATENT = 64
EXPERTS, HIDDEN = 4, 512
HCH = HIDDEN // P
FF1 = 384
FCH = FF1 // P
SCALE = float(HD) ** -0.5
PARTS = 3
PROD = PARTS * PARTS * HD
ROWS1 = 96
SHIFT = 96
ROWS2 = 98
LOWEST = -3.0e38
MASKED = -1.0e30

WCOLS = {}
_at = 0
for _n, _w in (("a_wq", 128), ("a_wk", 32), ("a_wv", 32), ("a_wo", 128),
               ("m_wq", 128), ("m_wqs", 128), ("m_wdkv", LATENT), ("m_wo", 128), ("gate", EXPERTS),
               ("b_wq", 128), ("b_wk", HD), ("b_wv", HD), ("b_wo", 128)):
    WCOLS[_n] = (_at, _at + _w)
    _at += _w
WN = _at
VCOLS = {n: i for i, n in enumerate(("a_bq", "a_bk", "norm1", "norm2", "ln_g", "ln_b", "b_bq", "b_bk", "b1"))}
VN = len(VCOLS) - 1 + EXPERTS * HCH
RCOLS = {}
_at = 0
for _n, _w in (("a_bv", 32), ("a_bo", 128), ("gate_b", EXPERTS), ("b2", EXPERTS * D), ("b_bv", HD), ("b_bo", 128)):
    RCOLS[_n] = (_at, _at + _w)
    _at += _w
RN = _at

PERIOD = 12
START = {"M": 3.0, "A": 7.0, "B": 23.0}
LAG = 1.8
CAUSAL_UNITS = 10
UNITS2 = {"M": CAUSAL_UNITS, "A": 16, "B": 16}
T = {"split_shift": 1.06, "turn_shift": 1.3, "pv": 2.2, "pvM": 3.2, "out_copy": 1.3, "out_turn": 0.2, "o_turn": 0.25,
     "o_proj": 0.15, "moe": 15.0, "up_step": 0.14, "ff": 1.0, "ff_step": 0.3, "x2n": 0.3, "x2s": 0.3, "ffd": 0.3}


def stages():
    out = []

    def put(t, name, *args):
        out.append((t, len(out), name, args))

    put(0.0, "x_norm")
    put(0.3, "x_scaled")
    put(0.5, "turn", "xr")
    put(0.6, "m_q")
    put(0.9, "m_lat")
    put(1.3, "m_lat_turn")
    put(1.5, "m_k")
    put(1.9, "m_v")
    put(0.8, "split", "mq")
    put(1.7, "split", "mk")
    put(2.0, "turn", "xn")
    put(2.5, "a_q")
    put(2.6, "split", "aq")
    put(3.3, "a_k")
    put(3.4, "split", "ak")
    put(3.7, "a_v")
    for a in "MAB":
        s = START[a]
        for g in range(GROUPS):
            for u in range(16):
                put(s + g + u / 16, "score_max", a, g, u)
            put(s + g + T["split_shift"], "shift_split", a, g)
            put(s + g + T["turn_shift"], "shift_turn", a, g)
            n = UNITS2[a]
            for u in range(n):
                put(s + LAG + g + (u + 0.5) / n, "score_exp", a, g, u)
                put(s + LAG + g + (u + 0.5 + T["pvM" if a == "M" else "pv"] * n / 16) / n, "probs_v", a, g, u)
            e = s + LAG + g + T["out_copy"]
            put(e, "out_copy", a, g)
            put(e + T["out_turn"], "out_turn", a, g)
    for a in "MAB":
        e = START[a] + LAG + 3 + T["out_copy"] + T["out_turn"] + T["o_turn"]
        put(e, "o_turn", a)
        put(e + T["o_proj"], "o_proj", a)
        if a == "M":
            put(e + T["o_proj"] + T["x2n"], "x2_norm")
    e0 = T["moe"]
    put(e0 - 0.7, "x2_scaled")
    put(e0 - 0.5, "turn", "r2")
    put(e0 - 0.2, "gate")
    step = T["up_step"]
    t = e0
    for e in range(EXPERTS):
        for c in range(HCH):
            put(t, "up", e, c)
            t += step
            if e and c in (1, 3):
                put(t - step / 2, "down", e - 1, c // 2)
                t += step
    put(t + 0.1, "down", EXPERTS - 1, 0)
    put(t + 0.2, "down", EXPERTS - 1, 1)
    for e in range(EXPERTS):
        put(e0 + 0.15 * e, "add_b2", e)
    b0 = t + 0.3
    put(b0, "x1_norm")
    put(b0 + 0.2, "x1_scaled")
    put(b0 + 0.4, "turn", "x1")
    put(b0 + 0.6, "b_q")
    put(b0 + 0.7, "split", "bq")
    put(b0 + 0.9, "b_k")
    put(b0 + 1.0, "split", "bk")
    put(b0 + 1.2, "b_v")
    f0 = b0 + T["ff"]
    for c in range(FCH):
        put(f0 + T["ff_step"] * c, "ff_up", c)
    put(f0 + T["ff_step"] * 2 + T["ffd"], "ff_down")
    out.sort()
    return out


def spare_users(name, *args):
    a, g = (args + (None, None))[:2]
    return {
        "turn": [(f"{a}_T", 1)], "m_q": [("rope_dve", 1), ("rope_dve", 2)], "m_lat": [("lat_copied", 1)],
        "m_lat_turn": [("latT_ready", 1)], "m_k": [("rope_dve", 3), ("rope_dve", 4)], "m_v": [("mv_ready", 1)],
        "a_q": [("aq_full", 1)], "a_k": [("ak_full", 1)], "a_v": [("av_ready", 1)],
        "b_q": [("bq_full", 1)], "b_k": [("bk_full", 1)], "b_v": [("bv_ready", 1)],
        "shift_turn": [(f"{a}_nmT", g + 1)] if name == "shift_turn" else [],
        "out_turn": [(f"{a}_otok", g + 1)] if name == "out_turn" else [],
        "o_turn": [(f"{a}_oT", 1)], "o_proj": [({"M": "x2_ready", "A": "gqa_added", "B": "y_ready"}.get(a), 1)],
        "gate": [("logits", 1)],
        "up": [("hid_act" if (HCH * a + g) % 2 else "hid_dve", (HCH * a + g) // 2 + 1)]
              if name == "up" else [],
        "down": [("acc_dve", 2 * a + g + 1)] if name == "down" else [],
        "ff_up": [("ff_gate", a + 1), ("ff_hid", a + 1)] if name == "ff_up" else [],
        "ff_down": [("res_b", 1)],
    }.get(name, [])


LAST = 2


def kernel_program(nc, x, w_all, w_lat, v_all, r_all, w1, w2, wi_up, wi_down, rope, out):
    table = sorted((t % PERIOD, order, name, args, int(t // PERIOD)) for t, order, name, args in stages())
    assert max(row[4] for row in table) == LAST

    q_parts = {a: nc.dram_tensor(f"q_parts_{a}", (PARTS, D, SEQ), BF16).ap() for a in "MBA"}
    kh = {"M": HEADS, "A": KV0, "B": 1}
    k_parts = {a: nc.dram_tensor(f"k_parts_{a}", (PARTS, kh[a] * HD, SEQ), BF16).ap() for a in "MBA"}

    nc.disable_value_cache = True
    ctx = ExitStack()
    with ctx:
        def sb(name, shape, dt=F32):
            return ctx.enter_context(nc.sbuf_tensor(name, shape, dt))

        def pb(name):
            return ctx.enter_context(nc.psum_tensor(name, [P, 512], F32))

        def sem(name):
            return ctx.enter_context(nc.semaphore(name))

        w = sb("w", [P, WN])
        wl = sb("wl", [P, 384])
        vec = sb("vec", [P, VN])
        row = sb("row", [P, RN])
        w1s = sb("w1s", [P, EXPERTS * HIDDEN])
        w2s = sb("w2s", [P, EXPERTS, HCH, D])
        wgu = sb("wgu", [P, 2 * FF1])
        wd = sb("wd", [P, FCH, D])
        rot = sb("rot", [P, 2, SEQ])
        ident = sb("ident", [P, P])
        identb = sb("identb", [P, P], BF16)
        mask = sb("mask", [P, SEQ])
        half_neg = sb("half_neg", [P, TILES])

        xs = sb("xs", [P, TILES, D])
        bn = sb("bn", [P, 2, TILES, 6])
        mv = sb("mv", [P, 2, TILES, 2])
        sq = sb("sq", [P, 7, TILES])
        sq2 = sb("sq2", [P, 4, TILES])
        sq1 = sb("sq1", [P, 2, TILES])
        xn = sb("xn", [P, TILES, D])
        factored = sb("factored", [P, TILES, D])
        xnT = sb("xnT", [P, SEQ])
        xrT = sb("xrT", [P, SEQ])
        res0 = sb("res0", [P, TILES, D])
        x2 = sb("x2", [P, TILES, D])
        r2T = sb("r2T", [P, SEQ])
        acc = sb("acc", [P, TILES, D])
        x1T = sb("x1T", [P, SEQ])
        res1 = sb("res1", [P, TILES, D])
        lat = sb("lat", [P, TILES, LATENT])
        latn = sb("latn", [P, TILES, LATENT])
        latT = sb("latT", [P, SEQ])
        lbn = sb("lbn", [P, TILES, 6])
        lmv = sb("lmv", [P, TILES, 2])
        lsq = sb("lsq", [P, 2, TILES])
        rope_s = sb("rope_s", [P, SEQ])
        full = {s: sb(f"full_{s}", [P, SEQ]) for s in "qk"}
        rest = sb("rest", [P, SEQ])
        parts = {s: sb(f"parts_{s}", [P, PARTS, SEQ], BF16) for s in "qk"}
        qp = {a: sb(f"qp_{a}", [P, HEADS, SEQ], BF16) for a in "MBA"}
        kp = {a: sb(f"kp_{a}", [P, kh[a], SEQ], BF16) for a in "MBA"}
        vv = {a: sb(f"vv_{a}", [P, TILES, kh[a], VW]) for a in "MBA"}
        mx = sb("mx", [P, 2, 16])
        junk = sb("junk", [P, 2, SEQ], BF16)
        nms = sb("nms", [P, 2, 2, 16], BF16)
        nmT = sb("nmT", [32, 2, P], BF16)
        NPR = 6
        probs = sb("probs", [P, NPR, SEQ])
        osb = sb("osb", [P, 2, SEQ])
        rc = sb("rc", [P, 2, 16])
        otok = sb("otok", [P, TILES, D])
        oT = sb("oT", [P, SEQ])
        lg = sb("lg", [P, TILES, EXPERTS])
        lmax = sb("lmax", [P, TILES])
        l1bn = sb("l1bn", [P, TILES, 6])
        l1mv = sb("l1mv", [P, TILES, 2])
        eq = sb("eq", [P, TILES, EXPERTS])
        seen = sb("seen", [P, 2, TILES])
        oneh = sb("oneh", [P, TILES, EXPERTS])
        NH = 8
        hid = sb("hid", [P, NH, SEQ])
        wi = hid[:, 0:3, :].rearrange("p c n -> p (c n)").bitcast(I32)
        th = sb("th", [P, SEQ])
        hf = sb("hf", [P, FCH, SEQ])

        s1 = [pb(f"s1_{i}") for i in range(2)]
        s2 = [pb(f"s2_{i}") for i in range(2)]
        pv = [pb(f"pv_{i}") for i in range(2)]
        misc = [pb(f"misc_{i}") for i in range(2)]

        sig, PER = {}, {}

        def declare(name, per):
            sig[name], PER[name] = sem(name), per

        ld_w, setup_dve, setup_pool, pool_chain = (
            sem(n) for n in ("ld_w", "setup_dve", "setup_pool", "pool_chain"))
        for name, per in (
                ("x_loaded", 16), ("x_bn", 1), ("x_stats", 1), ("x_rstd", 7), ("xn_ready", 1), ("xr_ready", 1),
                ("res0_ready", 1), ("turned_xr", 1), ("turned_xn", 1), ("turned_r2", 1), ("turned_x1", 1),
                ("xr_T", 1), ("xn_T", 1), ("r2_T", 1), ("x1_T", 1),
                ("mq_ps", 2), ("mk_ps", 2), ("rope_dve", 4), ("mq_full", 1), ("mk_full", 1),
                ("lat_ps", 1), ("lat_copied", 1), ("lat_bn", 1), ("lat_stats", 1), ("lat_rstd", 2),
                ("latn_ready", 1), ("latT_ps", 1), ("latT_ready", 1), ("mv_ps", 1), ("mv_ready", 1),
                ("a_ps", 3), ("aq_full", 1), ("ak_full", 1), ("av_ready", 1),
                ("b_ps", 3), ("bq_full", 1), ("bk_full", 1), ("bv_ready", 1),
                ("x2_ready", 1), ("x2_bn", 1), ("x2_stats", 1), ("x2_rstd", 4), ("r2_ready", 1),
                ("gate_ps", 1), ("logits", 1), ("top", 1), ("ties", 1), ("one_hot", 7), ("acc_base", 1 + EXPERTS), ("b2_term", EXPERTS),
                ("up_ps", 16), ("hid_act", 8), ("hid_dve", 8), ("down_ps", 8), ("acc_dve", 8),
                ("gqa_added", 1), ("x1_bn", 1), ("x1_stats", 1), ("x1_rstd", 2), ("x1n_ready", 1), ("res1_ready", 1),
                ("ff_ps", 2 * FCH), ("tanh_done", FCH), ("ff_gate", FCH), ("ff_hid", FCH), ("ffd_ps", 1), ("res_b", 1),
                ("y_ready", 1), ("y_stored", 16)):
            declare(name, per)
        for s in ("mq", "mk", "aq", "ak", "bq", "bk"):
            declare(f"{s}_split", 4)
            declare(f"{s}_stored", 16)
            declare(f"{s}_packed", 16 * (PARTS * PARTS))
        for a in "MBA":
            declare(f"{a}_s1_ps", 64)
            declare(f"{a}_s1_read", 64)
            declare(f"{a}_nms", 2 * GROUPS)
            declare(f"{a}_nmT_ps", GROUPS)
            declare(f"{a}_nmT", GROUPS)
            declare(f"{a}_shift", 32 * GROUPS)
            declare(f"{a}_s2_ps", GROUPS * UNITS2[a])
            declare(f"{a}_exp", GROUPS * UNITS2[a])
            declare(f"{a}_pv", GROUPS * UNITS2[a])
            declare(f"{a}_osb", GROUPS)
            declare(f"{a}_ot_ps", GROUPS)
            declare(f"{a}_rc", GROUPS)
            declare(f"{a}_otok", GROUPS)
            declare(f"{a}_oT_ps", 1)
            declare(f"{a}_oT", 1)
            declare(f"{a}_o_ps", 1)
        declare("M_masked", GROUPS * CAUSAL_UNITS)

        class At:

            def __init__(self, i, o):
                self.i, self.o = i, o
                self.first = isinstance(i, int) and i == o

            @property
            def prev(self):
                return At(self.i, self.o + 1)

        def total(b, name, k=None):
            per = PER[name]
            k = per if k is None else k
            return (b.i - b.o) * per + k if isinstance(b.i, int) else b.i * per + (k - b.o * per)

        names = [0]

        def in_register(eng, b, name, k=None):
            if isinstance(b.i, int):
                return total(b, name, k)
            per = PER[name]
            names[0] += 1
            with eng.register(f"past_{names[0]}") as past, eng.register(f"base_{names[0]}") as base, \
                    eng.register(f"value_{names[0]}") as value:
                eng.reg_add(past, b.i, -b.o)
                eng.reg_mul(base, past, per)
                eng.reg_add(value, base, per if k is None else k)
            return value

        def last_user(b, turn, key, name, k, eng=None):
            was = turn.get(key)
            turn[key] = (name, k, b.o)
            if was is None:
                return []
            n, kk, o = was
            at = At(b.i, o)
            return [(sig[n], total(at, n, kk) if eng is None else in_register(eng, at, n, kk))]

        def walk(eng, steps, turns):
            def iteration(i):
                for t in turns:
                    for key in t:
                        n, k, o = t[key]
                        t[key] = (n, k, o + 1)
                for _, _, name, args, o in table:
                    if name in steps and not (isinstance(i, int) and not 0 <= i - o < BATCH):
                        steps[name](At(i, o), *args)
            for i in range(LAST + 1):
                iteration(i)
            before = [dict(t) for t in turns]
            with eng.Fori(LAST + 1, BATCH) as i:
                iteration(i)
            assert before == [dict(t) for t in turns]
            for i in range(BATCH, BATCH + LAST):
                iteration(i)

        SPARE, SLOT = {}, {}
        for _, _, name, args, _ in table:
            for key in spare_users(name, *args):
                SPARE[key] = len(SPARE) % 2
            if name == "score_exp":
                SLOT[args] = len(SLOT) % NPR

        block = ctx.enter_context(nc.Block())

        def wc(name):
            return w[:, WCOLS[name][0]:WCOLS[name][1]]

        def rowv(name):
            return row[:, RCOLS[name][0]:RCOLS[name][1]]

        def vcol(name, n=P, k=0):
            return vec[0:n, VCOLS[name] + k:VCOLS[name] + k + 1]

        def spread(ap, n):
            return ap.unsqueeze(2).broadcast_to([ap.shape[0], ap.shape[1], n])

        def four(ap):
            return ap.rearrange("p (t d) -> p t d", t=TILES)

        def causal_parts(u):
            pair, r = divmod(u, 5)
            h0, h1 = 2 * pair, 2 * pair + 1
            if r in (0, 2):
                return [((h0, h1)[r // 2], 0, 0, 512)]
            if r in (1, 3):
                return [((h0, h1)[r // 2], 1, 0, 384), ((h0, h1)[r // 2], 3, 384, 128)]
            return [(h0, 2, 0, 256), (h1, 2, 256, 256)]

        def unit_parts(a, u):
            return causal_parts(u) if a == "M" else [(u // TILES, u % TILES, 0, SEQ)]

        def last_in_head(a, u, c):
            return c == (2 if a == "M" else TILES - 1)

        KHEAD = {"M": lambda h: h, "A": lambda h: h // (HEADS // KV0), "B": lambda h: 0}

        @block.sync
        def _(sp):
            for dst, src in ((w, w_all), (wl, w_lat), (vec, v_all), (w1s, w1), (w2s, w2), (rot, rope)):
                sp.dma_start(dst[:], src).then_inc(ld_w, 16)
            sp.dma_start(row[:], r_all.partition_broadcast(P)).then_inc(ld_w, 16)
            sp.dma_start(wi[:, 0:2 * FF1], wi_up).then_inc(ld_w, 16)
            sp.dma_start(wi[:, 2 * FF1:3 * FF1], wi_down).then_inc(ld_w, 16)
            sp.wait_ge(setup_pool, 1)

            def batch(ap, b):
                i = b.i if not b.o else b.i - b.o
                if isinstance(i, int):
                    return ap[i].rearrange("(t p) d -> p t d", p=P)
                return ap[bass.ds(i, 1)].rearrange("a (t p) d -> p (a t) d", p=P)

            def x_norm(b):
                if not b.first:
                    value = in_register(sp, b.prev, "xn_ready")
                    sp.wait_ge(setup_pool, 1)
                    sp.wait_ge(sig["xn_ready"], value)
                if not b.first:
                    value = in_register(sp, b.prev, "res0_ready")
                    sp.wait_ge(setup_pool, 1)
                    sp.wait_ge(sig["res0_ready"], value)
                sp.dma_start(xs[:], batch(x, b)).then_inc(sig["x_loaded"], 16)

            def shift_turn(b, a, g):
                value = in_register(sp, b, f"{a}_nmT", g + 1)
                sp.wait_ge(setup_pool, 1)
                sp.wait_ge(sig[f"{a}_nmT"], value)
                if g == 0:
                    if not b.first:
                        value = in_register(sp, b.prev, f"{a}_s2_ps")
                        sp.wait_ge(setup_pool, 1)
                        sp.wait_ge(sig[f"{a}_s2_ps"], value)
                for s in range(2):
                    sp.dma_start(qp[a][SHIFT + s:SHIFT + s + 1, GROUP * g:GROUP * g + GROUP, :],
                                        nmT[16 * s:16 * s + 16, g % 2, :]).then_inc(sig[f"{a}_shift"], 16)

            def split(b, s):
                a, is_q = s[0].upper(), s[1] == "q"
                n = HEADS * HD if is_q else kh[a] * HD
                scratch = q_parts[a] if is_q else k_parts[a]
                value = in_register(sp, b, f"{s}_split")
                sp.wait_ge(setup_pool, 1)
                sp.wait_ge(sig[f"{s}_split"], value)
                if not b.first:
                    value = in_register(sp, b.prev, f"{s}_packed")
                    sp.wait_ge(setup_pool, 1)
                    sp.wait_ge(sig[f"{s}_packed"], value)
                sp.dma_start(scratch.rearrange("s c n -> c s n"), parts[s[1]][0:n, :, :]).then_inc(sig[f"{s}_stored"], 16)
                value = in_register(sp, b, f"{s}_stored")
                sp.wait_ge(setup_pool, 1)
                sp.wait_ge(sig[f"{s}_stored"], value)
                if not b.first:
                    value = in_register(sp, b.prev, f"{a}_s2_ps")
                    sp.wait_ge(setup_pool, 1)
                    sp.wait_ge(sig[f"{a}_s2_ps"], value)
                if not b.first:
                    value = in_register(sp, b.prev, f"{a}_s1_ps")
                    sp.wait_ge(setup_pool, 1)
                    sp.wait_ge(sig[f"{a}_s1_ps"], value)
                for i in range(PARTS):
                    for j in range(PARTS):
                        r = (PARTS * i + j) * HD
                        sp.dma_start((qp if is_q else kp)[a][r:r + HD, :, :],
                                            scratch[i if is_q else j].rearrange("(h d) n -> d h n", d=HD)).then_inc(sig[f"{s}_packed"], 16)

            def o_proj(b, a):
                if a == "B":
                    value = in_register(sp, b, "y_ready")
                    sp.wait_ge(setup_pool, 1)
                    sp.wait_ge(sig["y_ready"], value)
                    sp.dma_start(batch(out, b), res1[:]).then_inc(sig["y_stored"], 16)

            walk(sp, {"x_norm": x_norm, "shift_turn": shift_turn, "split": split, "o_proj": o_proj}, [])
            sp.wait_ge(sig["y_stored"], 16 * BATCH)

        @block.tensor
        def _(pe):
            banks = {}
            pe.wait_ge(ld_w, 16 * 9)
            pe.wait_ge(setup_pool, 1)
            pe.wait_ge(setup_dve, 3)
            turn_misc, turn_s1, turn_s2, turn_pv = {}, {}, {}, {}

            def misc_bank(b, name, k):
                m = SPARE[name, k]
                for s_last, value in last_user(b, turn_misc, m, name, k):
                    pe.wait_ge(s_last, value)
                return misc[m]

            def turns4(dst, src, name):
                for t in range(TILES):
                    ins = pe.transpose(dst[:, P * t:P * t + P], src[:, t, :], ident[:])
                ins.then_inc(sig[name], 1)

            def turn(b, what):
                src, ready, done = {"xr": (factored, "xr_ready", "xr_T"), "xn": (xn, "xn_ready", "xn_T"),
                                    "r2": (factored, "r2_ready", "r2_T"), "x1": (factored, "x1n_ready", "x1_T")}[what]
                m = misc_bank(b, done, 1)
                pe.wait_ge(sig[ready], total(b, ready))
                turns4(m, src, "turned_" + what)

            def dense(m, n, lhsT, rhs, name):
                pe.matmul(m[0:n, :], lhsT, rhs, start=True, stop=True).then_inc(sig[name], 1)

            def m_q(b):
                pe.wait_ge(sig["xr_T"], total(b, "xr_T"))
                for j, wn in enumerate(("m_wq", "m_wqs")):
                    dense(misc_bank(b, "rope_dve", 1 + j), P, wc(wn), xrT[:], "mq_ps")

            def m_lat(b):
                pe.wait_ge(sig["xr_T"], total(b, "xr_T"))
                m = misc_bank(b, "lat_copied", 1)
                for t in range(TILES):
                    ins = pe.matmul(m[:, LATENT * t:LATENT * t + LATENT], xrT[:, P * t:P * t + P], wc("m_wdkv"),
                                    start=True, stop=True)
                ins.then_inc(sig["lat_ps"], 1)

            def m_lat_turn(b):
                m = misc_bank(b, "latT_ready", 1)
                value = in_register(pe, b, "latn_ready")
                pe.wait_ge(setup_pool, 1)
                pe.wait_ge(sig["latn_ready"], value)
                for t in range(TILES):
                    ins = pe.transpose(m[0:LATENT, P * t:P * t + P], latn[:, t, :], ident[:])
                ins.then_inc(sig["latT_ps"], 1)

            def m_k(b):
                pe.wait_ge(sig["latT_ready"], total(b, "latT_ready"))
                for j in range(2):
                    dense(misc_bank(b, "rope_dve", 3 + j), P, wl[:, P * j:P * j + P], latT[:], "mk_ps")

            def values(b, src, weight, width, done, name):
                m = misc_bank(b, done, 1)
                for t in range(TILES):
                    ins = pe.matmul(m[:, width * t:width * t + width], src[:, P * t:P * t + P], weight,
                                    start=True, stop=True)
                ins.then_inc(sig[name], 1)

            def m_v(b):
                values(b, latT, wl[:, 2 * P:3 * P], P, "mv_ready", "mv_ps")

            def a_q(b):
                pe.wait_ge(sig["xn_T"], total(b, "xn_T"))
                dense(misc_bank(b, "aq_full", 1), P, wc("a_wq"), xnT[:], "a_ps")

            def a_k(b):
                dense(misc_bank(b, "ak_full", 1), KV0 * HD, wc("a_wk"), xnT[:], "a_ps")

            def a_v(b):
                values(b, xnT, wc("a_wv"), KV0 * HD, "av_ready", "a_ps")

            def b_q(b):
                pe.wait_ge(sig["x1_T"], total(b, "x1_T"))
                dense(misc_bank(b, "bq_full", 1), P, wc("b_wq"), x1T[:], "b_ps")

            def b_k(b):
                dense(misc_bank(b, "bk_full", 1), HD, wc("b_wk"), x1T[:], "b_ps")

            def b_v(b):
                values(b, x1T, wc("b_wv"), HD, "bv_ready", "b_ps")

            def score_max(b, a, g, u):
                n = 16 * g + u
                if n == 0:
                    low = a.lower()
                    pe.wait_ge(sig[f"{low}q_packed"], total(b, f"{low}q_packed"))
                    pe.wait_ge(sig[f"{low}k_packed"], total(b, f"{low}k_packed"))
                h, t = GROUP * g + u // TILES, u % TILES
                keys = P * (t + 1) if a == "M" else SEQ
                for s_last, value in last_user(b, turn_s1, n % 2, f"{a}_s1_read", n + 1):
                    pe.wait_ge(s_last, value)
                pe.matmul(s1[n % 2][:, 0:keys], qp[a][0:ROWS1, h, P * t:P * t + P],
                                 kp[a][0:ROWS1, KHEAD[a](h), 0:keys], start=True, stop=True).then_inc(sig[f"{a}_s1_ps"], 1)

            def shift_turn(b, a, g):
                m = misc_bank(b, f"{a}_nmT", g + 1)
                pe.wait_ge(sig[f"{a}_nms"], total(b, f"{a}_nms", 2 * g + 2))
                mb = m[:].bitcast(BF16)
                pe.transpose(mb[0:32, 0:P], nms[:, g % 2].rearrange("p s n -> p (s n)"), identb[:]).then_inc(sig[f"{a}_nmT_ps"], 1)

            def score_exp(b, a, g, u):
                n = UNITS2[a] * g + u
                if u == 0:
                    pe.wait_ge(sig[f"{a}_shift"], total(b, f"{a}_shift", 32 * (g + 1)))
                for s_last, value in last_user(b, turn_s2, n % 2, f"{a}_exp", n + 1):
                    pe.wait_ge(s_last, value)
                for hh, c, col, q in unit_parts(a, u):
                    h = GROUP * g + hh
                    ins = pe.matmul(s2[n % 2][:, col:col + q], kp[a][0:ROWS2, KHEAD[a](h), P * c:P * c + P],
                                    qp[a][0:ROWS2, h, SEQ - q:SEQ], start=True, stop=True)
                ins.then_inc(sig[f"{a}_s2_ps"], 1)

            def probs_v(b, a, g, u):
                n = UNITS2[a] * g + u
                pe.wait_ge(sig["M_masked" if a == "M" else f"{a}_exp"], total(b, "M_masked" if a == "M" else f"{a}_exp", n + 1))
                if n == 0:
                    pe.wait_ge(sig[{"M": "mv_ready", "A": "av_ready", "B": "bv_ready"}[a]], total(b, {"M": "mv_ready", "A": "av_ready", "B": "bv_ready"}[a]))
                if u == 0:
                    for s_last, value in last_user(b, turn_pv, g % 2, f"{a}_osb", g + 1):
                        pe.wait_ge(s_last, value)
                slot = SLOT[a, g, u]
                for hh, c, col, q in unit_parts(a, u):
                    ins = pe.matmul(pv[g % 2][32 * hh:32 * hh + VW, SEQ - q:SEQ],
                                    vv[a][:, c, KHEAD[a](GROUP * g + hh), :], probs[:, slot, col:col + q],
                                    start=(c == 0), stop=last_in_head(a, u, c), tile_position=(0, 32 * hh))
                ins.then_inc(sig[f"{a}_pv"], 1)

            def out_turn(b, a, g):
                m = misc_bank(b, f"{a}_otok", g + 1)
                pe.wait_ge(sig[f"{a}_osb"], total(b, f"{a}_osb", g + 1))
                for t in range(TILES):
                    ins = pe.transpose(m[:, P * t:P * t + P], osb[:, g % 2, P * t:P * t + P], ident[:])
                ins.then_inc(sig[f"{a}_ot_ps"], 1)

            def o_turn(b, a):
                m = misc_bank(b, f"{a}_oT", 1)
                pe.wait_ge(sig[f"{a}_otok"], total(b, f"{a}_otok"))
                turns4(m, otok, f"{a}_oT_ps")

            def o_proj(b, a):
                m = misc_bank(b, {"M": "x2_ready", "A": "gqa_added", "B": "y_ready"}[a], 1)
                pe.wait_ge(sig[f"{a}_oT"], total(b, f"{a}_oT"))
                for t in range(TILES):
                    ins = pe.matmul(m[:, P * t:P * t + P], oT[:, P * t:P * t + P], wc(f"{a.lower()}_wo"),
                                    start=True, stop=True)
                ins.then_inc(sig[f"{a}_o_ps"], 1)

            def gate(b):
                m = misc_bank(b, "logits", 1)
                pe.wait_ge(sig["r2_T"], total(b, "r2_T"))
                for t in range(TILES):
                    ins = pe.matmul(m[:, EXPERTS * t:EXPERTS * t + EXPERTS], r2T[:, P * t:P * t + P], wc("gate"),
                                    start=True, stop=True)
                ins.then_inc(sig["gate_ps"], 1)

            def up(b, e, c):
                n = HCH * e + c
                m = misc_bank(b, "hid_act" if n % 2 else "hid_dve", n // 2 + 1)
                pe.matmul(m[:], w1s[:, P * n:P * n + P], r2T[:], start=True, stop=True).then_inc(sig["up_ps"], 1)

            def down(b, e, half):
                m = misc_bank(b, "acc_dve", 2 * e + half + 1)
                pe.wait_ge(sig["hid_act"], total(b, "hid_act", 2 * e + 2))
                pe.wait_ge(sig["hid_dve"], total(b, "hid_dve", 2 * e + 2))
                for t in range(2 * half, 2 * half + 2):
                    for c in range(HCH):
                        ins = pe.matmul(m[:, P * (t % 2):P * (t % 2) + P],
                                        hid[:, (HCH * e + c) % NH, P * t:P * t + P], w2s[:, e, c, :],
                                        start=(c == 0), stop=(c == HCH - 1))
                ins.then_inc(sig["down_ps"], 1)

            def ff_up(b, c):
                for j in range(2):
                    dense(misc_bank(b, "ff_gate" if j == 0 else "ff_hid", c + 1), P,
                          wgu[:, FF1 * j + P * c:FF1 * j + P * c + P], x1T[:], "ff_ps")

            def ff_down(b):
                m = misc_bank(b, "res_b", 1)
                pe.wait_ge(sig["ff_hid"], total(b, "ff_hid"))
                for t in range(TILES):
                    for c in range(FCH):
                        ins = pe.matmul(m[:, P * t:P * t + P], hf[:, c, P * t:P * t + P], wd[:, c, :],
                                        start=(c == 0), stop=(c == FCH - 1))
                ins.then_inc(sig["ffd_ps"], 1)

            steps = dict(turn=turn, m_q=m_q, m_lat=m_lat, m_lat_turn=m_lat_turn, m_k=m_k, m_v=m_v,
                         a_q=a_q, a_k=a_k, a_v=a_v, b_q=b_q, b_k=b_k, b_v=b_v, score_max=score_max,
                         shift_turn=shift_turn, score_exp=score_exp, probs_v=probs_v, out_turn=out_turn,
                         o_turn=o_turn, o_proj=o_proj, gate=gate, up=up, down=down, ff_up=ff_up, ff_down=ff_down)
            walk(pe, steps, [turn_misc, turn_s1, turn_s2, turn_pv])

        @block.vector
        def _(v):
            turn_mx, turn_nmT, turn_factored, turn_full, turn_otok = {}, {}, {}, {}, {}
            v.memset(half_neg[:], -0.5).then_inc(setup_dve, 1)
            v.wait_ge(ld_w, 16 * 9)
            v.tensor_scalar(wgu[:], wi[:, 0:2 * FF1], 1.0 / 127.0, None, ALU.mult).then_inc(setup_dve, 1)
            v.tensor_scalar(wd[:].rearrange("p c d -> p (c d)"), wi[:, 2 * FF1:3 * FF1], 1.0 / 127.0, 0.5,
                            ALU.mult, ALU.mult).then_inc(setup_dve, 1)
            v.wait_ge(setup_pool, 1)

            def stats(b, src, bns, mvs, chain, done):
                for t in range(TILES):
                    ins = v.bn_stats(bns[:, t, :], src[:, t, :])
                ins.then_inc(sig[chain], 1)
                value = in_register(v, b, chain)
                v.wait_ge(setup_pool, 1)
                v.wait_ge(sig[chain], value)
                for t in range(TILES):
                    ins = v.bn_aggr(mvs[:, t, :], bns[:, t, :])
                ins.then_inc(sig[done], 1)

            def normed(dst, src, mvs, rstd, name):
                for t in range(TILES):
                    ins = v.tensor_scalar(dst[:, t, :], src[:, t, :], mvs[:, t, 0:1], rstd[:, t:t + 1],
                                          ALU.subtract, ALU.mult)
                ins.then_inc(sig[name], 1)

            def scaled(dst, src, factor, name):
                for t in range(TILES):
                    ins = v.tensor_scalar(dst[:, t, :], src[:, t, :], factor[:, t:t + 1], None, ALU.mult)
                ins.then_inc(sig[name], 1)

            def x_norm(b):
                v.wait_ge(sig["x_loaded"], total(b, "x_loaded"))
                if not b.first:
                    v.wait_ge(sig["x_rstd"], total(b.prev, "x_rstd"))
                stats(b, xs, bn[:, 0], mv[:, 0], "x_bn", "x_stats")

            def x_scaled(b):
                v.wait_ge(sig["x_rstd"], total(b, "x_rstd"))
                if not b.first:
                    v.wait_ge(sig["turned_xn"], total(b.prev, "turned_xn"))
                if not b.first:
                    v.wait_ge(sig["x2_ready"], total(b.prev, "x2_ready"))
                normed(xn, xs, mv[:, 0], sq[:, 1], "xn_ready")
                v.wait_ge(sig["xn_ready"], total(b, "xn_ready"))
                for s_last, value in last_user(b, turn_factored, 0, "turned_xr", 1):
                    v.wait_ge(s_last, value)
                scaled(factored, xn, sq[:, 6], "xr_ready")

            def turn(b, what):
                if what == "xr":
                    v.wait_ge(sig["turned_xr"], total(b, "turned_xr"))
                    if not b.first:
                        v.wait_ge(sig["mq_ps"], total(b.prev, "mq_ps"))
                    if not b.first:
                        v.wait_ge(sig["lat_ps"], total(b.prev, "lat_ps"))
                    v.tensor_scalar(xrT[:], misc[SPARE["xr_T", 1]][:], vcol("norm1"), None, ALU.mult).then_inc(sig["xr_T"], 1)
                if what == "r2":
                    v.wait_ge(sig["turned_r2"], total(b, "turned_r2"))
                    if not b.first:
                        v.wait_ge(sig["up_ps"], total(b.prev, "up_ps"))
                    v.tensor_scalar(r2T[:], misc[SPARE["r2_T", 1]][:], vcol("norm2"), None, ALU.mult).then_inc(sig["r2_T"], 1)

            def rope_mul(b, s, first, factor):
                for s_last, value in last_user(b, turn_full, s[1], f"{s}_split", 4):
                    v.wait_ge(s_last, value)
                for j, dst in enumerate((full[s[1]], rope_s)):
                    v.wait_ge(sig[f"{s}_ps"], total(b, f"{s}_ps", j + 1))
                    if j:
                        for s_last, value in last_user(b, turn_full, "rope_s", f"{s}_full", 1):
                            v.wait_ge(s_last, value)
                    v.scalar_tensor_tensor(out=dst[:], in0=misc[SPARE["rope_dve", first + j]][:],
                                                  scalar=factor, in1=rot[:, j, :], op0=ALU.mult, op1=ALU.mult).then_inc(sig["rope_dve"], 1)

            def m_q(b):
                rope_mul(b, "mq", 1, SCALE)

            def m_k(b):
                rope_mul(b, "mk", 3, 1.0)

            def m_lat(b):
                v.wait_ge(sig["lat_ps"], total(b, "lat_ps"))
                if not b.first:
                    v.wait_ge(sig["latn_ready"], total(b.prev, "latn_ready"))
                v.tensor_copy(lat[:].rearrange("p t n -> p (t n)"),
                                     misc[SPARE["lat_copied", 1]][:, 0:TILES * LATENT]).then_inc(sig["lat_copied"], 1)
                v.wait_ge(sig["lat_copied"], total(b, "lat_copied"))
                if not b.first:
                    v.wait_ge(sig["lat_rstd"], total(b.prev, "lat_rstd"))
                stats(b, lat, lbn, lmv, "lat_bn", "lat_stats")

            def m_lat_turn(b):
                v.wait_ge(sig["lat_rstd"], total(b, "lat_rstd"))
                if not b.first:
                    v.wait_ge(sig["latT_ps"], total(b.prev, "latT_ps"))
                normed(latn, lat, lmv, lsq[:, 1], "latn_ready")
                v.wait_ge(sig["latT_ps"], total(b, "latT_ps"))
                if not b.first:
                    v.wait_ge(sig["mv_ps"], total(b.prev, "mv_ps"))
                v.tensor_scalar(latT[0:LATENT, :], misc[SPARE["latT_ready", 1]][0:LATENT, :],
                                       vcol("ln_g", LATENT), vcol("ln_b", LATENT), ALU.mult, ALU.add).then_inc(sig["latT_ready"], 1)

            def query(b, s, ps, bias):
                v.wait_ge(sig[ps], total(b, ps, 1))
                for s_last, value in last_user(b, turn_full, s[1], f"{s}_split", 4):
                    v.wait_ge(s_last, value)
                v.tensor_scalar(full[s[1]][:], misc[SPARE[f"{s}_full", 1]][:], vcol(bias), SCALE,
                                       ALU.add, ALU.mult).then_inc(sig[f"{s}_full"], 1)

            def key(b, s, ps, bias, n):
                v.wait_ge(sig[ps], total(b, ps, 2))
                for s_last, value in last_user(b, turn_full, s[1], f"{s}_split", 4):
                    v.wait_ge(s_last, value)
                v.tensor_scalar(full[s[1]][0:n, :], misc[SPARE[f"{s}_full", 1]][0:n, :], vcol(bias, n), None,
                                       ALU.add).then_inc(sig[f"{s}_full"], 1)

            def value(b, a, ps, bias, done):
                n = kh[a]
                v.wait_ge(sig[ps], total(b, ps, 3))
                if not b.first:
                    v.wait_ge(sig[f"{a}_pv"], total(b.prev, f"{a}_pv"))
                src = misc[SPARE[done, 1]][:, 0:TILES * n * HD].rearrange("p (t h d) -> p t h d", t=TILES, d=HD)
                bv = rowv(bias).rearrange("p (h d) -> p h d", d=HD).unsqueeze(1).broadcast_to([P, TILES, n, HD])
                v.tensor_tensor(vv[a][:, :, :, 0:HD], src, bv, ALU.add).then_inc(sig[done], 1)

            def score_max(b, a, g, u):
                n = 16 * g + u
                if u == 0:
                    for s_last, value in last_user(b, turn_mx, g % 2, f"{a}_nms", 2 * g + 2):
                        v.wait_ge(s_last, value)
                if a == "M":
                    if n >= 2:
                        if not b.first or n > 1:
                            value = in_register(v, b, "M_s1_read", n - 1)
                            v.wait_ge(setup_pool, 1)
                            v.wait_ge(sig["M_s1_read"], value)
                    value = in_register(v, b, "M_s1_ps", n + 1)
                    v.wait_ge(setup_pool, 1)
                    v.wait_ge(sig["M_s1_ps"], value)
                else:
                    v.wait_ge(sig[f"{a}_s1_ps"], total(b, f"{a}_s1_ps", n + 1))
                dst = mx[:, g % 2, u:u + 1]
                if a == "M":
                    keys = P * (u % TILES + 1)
                    ins = v.tensor_tensor_reduce(junk[:, n % 2, 0:keys], s1[n % 2][:, 0:keys],
                                                 mask[:, SEQ - keys:SEQ], 1.0, LOWEST, ALU.add, ALU.max, dst)
                else:
                    ins = v.tensor_reduce(dst, s1[n % 2][:], AX.X, ALU.max)
                ins.then_inc(sig[f"{a}_s1_read"], 1)

            def shift_turn(b, a, g):
                for s_last, value in last_user(b, turn_nmT, g % 2, f"{a}_shift", 32 * (g + 1)):
                    v.wait_ge(s_last, value)
                v.wait_ge(sig[f"{a}_nmT_ps"], total(b, f"{a}_nmT_ps", g + 1))
                v.tensor_copy(nmT[:, g % 2, :], misc[SPARE[f"{a}_nmT", g + 1]][:].bitcast(BF16)[0:32, 0:P]).then_inc(sig[f"{a}_nmT"], 1)

            def out_turn(b, a, g):
                v.wait_ge(sig[f"{a}_ot_ps"], total(b, f"{a}_ot_ps", g + 1))
                m = misc[SPARE[f"{a}_otok", g + 1]][:].rearrange("p (t h c) -> p t h c", t=TILES, h=GROUP)
                r = rc[:, g % 2, :].rearrange("p (t h) -> p t h", t=TILES)
                v.reciprocal(r, m[:, :, :, HD]).then_inc(sig[f"{a}_rc"], 1)
                v.wait_ge(sig[f"{a}_rc"], total(b, f"{a}_rc", g + 1))
                if g == 0:
                    for s_last, value in last_user(b, turn_otok, 0, f"{a}_oT_ps", 1):
                        v.wait_ge(s_last, value)
                dst = otok[:, :, GROUP * HD * g:GROUP * HD * (g + 1)].rearrange("p t (h d) -> p t h d", h=GROUP)
                v.tensor_tensor(dst, m[:, :, :, 0:HD],
                                       r.unsqueeze(3).broadcast_to([P, TILES, GROUP, HD]), ALU.mult).then_inc(sig[f"{a}_otok"], 1)

            def o_proj(b, a):
                v.wait_ge(sig[f"{a}_o_ps"], total(b, f"{a}_o_ps"))
                if a == "M":
                    if not b.first:
                        v.wait_ge(sig["r2_ready"], total(b.prev, "r2_ready"))
                    if not b.first:
                        v.wait_ge(sig["acc_base"], total(b.prev, "acc_base", 1))
                    m = misc[SPARE["x2_ready", 1]][:]
                    v.tensor_tensor(x2[:], four(m), xn[:], ALU.add).then_inc(sig["x2_ready"], 1)
                if a == "A":
                    v.wait_ge(sig["acc_base"], total(b, "acc_base", 1))
                    m = misc[SPARE["gqa_added", 1]][:]
                    v.tensor_tensor(acc[:], four(m), acc[:], ALU.add).then_inc(sig["gqa_added"], 1)
                if a == "B":
                    v.wait_ge(sig["res_b"], total(b, "res_b"))
                    m = misc[SPARE["y_ready", 1]][:]
                    v.tensor_tensor(res1[:], four(m), res1[:], ALU.add).then_inc(sig["y_ready"], 1)

            def x2_norm(b):
                v.wait_ge(sig["x2_ready"], total(b, "x2_ready"))
                if not b.first:
                    v.wait_ge(sig["x2_rstd"], total(b.prev, "x2_rstd"))
                stats(b, x2, bn[:, 1], mv[:, 1], "x2_bn", "x2_stats")

            def x2_scaled(b):
                v.wait_ge(sig["x2_rstd"], total(b, "x2_rstd"))
                for s_last, value in last_user(b, turn_factored, 0, "turned_r2", 1):
                    v.wait_ge(s_last, value)
                scaled(factored, x2, sq2[:, 3], "r2_ready")

            def gate(b):
                v.wait_ge(sig["gate_ps"], total(b, "gate_ps"))
                if not b.first:
                    v.wait_ge(sig["one_hot"], total(b.prev, "one_hot"))
                m = misc[SPARE["logits", 1]][:, 0:TILES * EXPERTS].rearrange("p (t e) -> p t e", t=TILES)
                v.tensor_tensor(lg[:], m, rowv("gate_b").unsqueeze(1).broadcast_to([P, TILES, EXPERTS]),
                                       ALU.add).then_inc(sig["logits"], 1)
                v.wait_ge(sig["logits"], total(b, "logits"))
                v.tensor_reduce(lmax[:], lg[:], AX.X, ALU.max).then_inc(sig["top"], 1)
                v.wait_ge(sig["top"], total(b, "top"))
                v.tensor_tensor(eq[:], lg[:], spread(lmax[:], EXPERTS), ALU.is_equal).then_inc(sig["ties"], 1)

            def up(b, e, c):
                n = HCH * e + c
                if n % 2:
                    return
                v.wait_ge(sig["up_ps"], total(b, "up_ps", n + 1))
                if not b.first or e > 1:
                    v.wait_ge(sig["down_ps"], total(b, "down_ps", 2 * e - 2))
                v.tensor_scalar(hid[:, n % NH, :], misc[SPARE["hid_dve", n // 2 + 1]][:],
                                       vcol("b1", k=n), 0.0, ALU.add, ALU.max).then_inc(sig["hid_dve"], 1)

            def down(b, e, half):
                n = 2 * e + half
                v.wait_ge(sig["down_ps"], total(b, "down_ps", n + 1))
                v.wait_ge(sig["acc_base"], total(b, "acc_base"))
                if not b.first or n > 1:
                    v.wait_ge(sig["acc_dve"], total(b, "acc_dve", n - 1))
                m = misc[SPARE["acc_dve", n + 1]]
                for j in range(2):
                    t = 2 * half + j
                    ins = v.scalar_tensor_tensor(out=acc[:, t, :], in0=m[:, P * j:P * j + P],
                                                 scalar=oneh[:, t, e:e + 1], in1=acc[:, t, :],
                                                 op0=ALU.mult, op1=ALU.add)
                ins.then_inc(sig["acc_dve"], 1)

            def x1_norm(b):
                v.wait_ge(sig["acc_dve"], total(b, "acc_dve"))
                if not b.first:
                    v.wait_ge(sig["x1_rstd"], total(b.prev, "x1_rstd"))
                stats(b, acc, l1bn, l1mv, "x1_bn", "x1_stats")

            def x1_scaled(b):
                v.wait_ge(sig["x1_rstd"], total(b, "x1_rstd"))
                for s_last, value in last_user(b, turn_factored, 0, "turned_x1", 1):
                    v.wait_ge(s_last, value)
                normed(factored, acc, l1mv, sq1[:, 1], "x1n_ready")

            def ff_up(b, c):
                v.wait_ge(sig["tanh_done"], total(b, "tanh_done", c + 1))
                v.scalar_tensor_tensor(out=th[:], in0=th[:], scalar=1.0, in1=misc[SPARE["ff_gate", c + 1]][:],
                                              op0=ALU.add, op1=ALU.mult).then_inc(sig["ff_gate"], 1)
                v.wait_ge(sig["ff_gate"], total(b, "ff_gate", c + 1))
                v.wait_ge(sig["ff_ps"], total(b, "ff_ps", 2 * c + 2))
                if not b.first:
                    v.wait_ge(sig["ffd_ps"], total(b.prev, "ffd_ps"))
                v.tensor_tensor(hf[:, c, :], th[:], misc[SPARE["ff_hid", c + 1]][:], ALU.mult).then_inc(sig["ff_hid"], 1)

            def ff_down(b):
                v.wait_ge(sig["ffd_ps"], total(b, "ffd_ps"))
                v.wait_ge(sig["res1_ready"], total(b, "res1_ready"))
                v.tensor_tensor(res1[:], four(misc[SPARE["res_b", 1]][:]), res1[:], ALU.add).then_inc(sig["res_b"], 1)

            steps = dict(x_norm=x_norm, x_scaled=x_scaled, turn=turn, m_q=m_q, m_k=m_k, m_lat=m_lat,
                         m_lat_turn=m_lat_turn,
                         a_q=lambda b: query(b, "aq", "a_ps", "a_bq"),
                         a_k=lambda b: key(b, "ak", "a_ps", "a_bk", KV0 * HD),
                         a_v=lambda b: value(b, "A", "a_ps", "a_bv", "av_ready"),
                         b_q=lambda b: query(b, "bq", "b_ps", "b_bq"),
                         b_k=lambda b: key(b, "bk", "b_ps", "b_bk", HD),
                         b_v=lambda b: value(b, "B", "b_ps", "b_bv", "bv_ready"),
                         score_max=score_max, shift_turn=shift_turn, out_turn=out_turn, o_proj=o_proj,
                         x2_norm=x2_norm, x2_scaled=x2_scaled, gate=gate, up=up, down=down,
                         x1_norm=x1_norm, x1_scaled=x1_scaled, ff_up=ff_up, ff_down=ff_down)
            walk(v, steps, [turn_mx, turn_nmT, turn_factored, turn_full, turn_otok])

        @block.scalar
        def _(act):
            turn_probs, turn_osb, turn_oT = {}, {}, {}
            act.wait_ge(ld_w, 16 * 9)
            act.wait_ge(setup_pool, 1)

            def turn(b, what):
                if what in ("xn", "x1"):
                    dst = {"xn": xnT, "x1": x1T}[what]
                    act.wait_ge(sig["turned_" + what], total(b, "turned_" + what))
                    for reader in {"xn": ("a_ps",), "x1": ("b_ps", "ff_ps")}[what]:
                        if not b.first:
                            act.wait_ge(sig[reader], total(b.prev, reader))
                    act.activation(dst[:], misc[SPARE[what + "_T", 1]][:], ACT.Copy).then_inc(sig[what + "_T"], 1)

            def m_v(b):
                act.wait_ge(sig["mv_ps"], total(b, "mv_ps"))
                if not b.first:
                    act.wait_ge(sig["M_pv"], total(b.prev, "M_pv"))
                dst = vv["M"][:].rearrange("p t h c -> p (t h) c")[:, :, 0:HD]
                act.activation(dst, misc[SPARE["mv_ready", 1]][:].rearrange("p (n d) -> p n d", d=HD),
                                      ACT.Copy).then_inc(sig["mv_ready"], 1)

            def score_exp(b, a, g, u):
                n = UNITS2[a] * g + u
                act.wait_ge(sig[f"{a}_s2_ps"], total(b, f"{a}_s2_ps", n + 1))
                slot = SLOT[a, g, u]
                for s_last, value in last_user(b, turn_probs, slot, f"{a}_pv", n + 1):
                    act.wait_ge(s_last, value)
                act.activation(probs[:, slot, :], s2[n % 2][:], ACT.Exp).then_inc(sig[f"{a}_exp"], 1)

            def out_copy(b, a, g):
                act.wait_ge(sig[f"{a}_pv"], total(b, f"{a}_pv", UNITS2[a] * (g + 1)))
                for s_last, value in last_user(b, turn_osb, g % 2, f"{a}_ot_ps", g + 1):
                    act.wait_ge(s_last, value)
                act.activation(osb[:, g % 2, :], pv[g % 2][:], ACT.Copy).then_inc(sig[f"{a}_osb"], 1)

            def o_turn(b, a):
                act.wait_ge(sig[f"{a}_oT_ps"], total(b, f"{a}_oT_ps"))
                for s_last, value in last_user(b, turn_oT, 0, f"{a}_o_ps", 1):
                    act.wait_ge(s_last, value)
                act.activation(oT[:], misc[SPARE[f"{a}_oT", 1]][:], ACT.Copy).then_inc(sig[f"{a}_oT"], 1)

            def up(b, e, c):
                n = HCH * e + c
                if n % 2 == 0:
                    return
                act.wait_ge(sig["up_ps"], total(b, "up_ps", n + 1))
                if not b.first or e > 1:
                    act.wait_ge(sig["down_ps"], total(b, "down_ps", 2 * e - 2))
                act.activation(hid[:, n % NH, :], misc[SPARE["hid_act", n // 2 + 1]][:], ACT.Relu,
                                      bias=vcol("b1", k=n)).then_inc(sig["hid_act"], 1)

            def ff_up(b, c):
                act.wait_ge(sig["ff_ps"], total(b, "ff_ps", 2 * c + 1))
                if not b.first or c:
                    act.wait_ge(sig["ff_hid"], total(b, "ff_hid", c))
                act.activation(th[:], misc[SPARE["ff_gate", c + 1]][:], ACT.Tanh, scale=0.5).then_inc(sig["tanh_done"], 1)

            walk(act, dict(turn=turn, m_v=m_v, score_exp=score_exp, out_copy=out_copy, o_turn=o_turn, up=up,
                           ff_up=ff_up), [turn_probs, turn_osb, turn_oT])

        @block.gpsimd
        def _(pool):
            turn_nms, turn_parts = {}, {}
            done = [0]

            def link(ins):
                done[0] += 1
                ins.then_inc(pool_chain, 1)
                pool.wait_ge(pool_chain, done[0])

            for m in (ident, identb):
                link(pool.memset(m[:], 0.0))
                link(pool.affine_select(out=m[:], in_=m[:], compare_op=ALU.not_equal, fill=1.0, base=0,
                                        pattern=[[-1, P]], channel_multiplier=1))
            link(pool.memset(mask[:], 0.0))
            link(pool.affine_select(out=mask[:, SEQ - P:SEQ], in_=mask[:, SEQ - P:SEQ], compare_op=ALU.is_ge,
                                    fill=MASKED, base=0, pattern=[[-1, P]], channel_multiplier=1))
            link(pool.memset(latT[:], 0.0))
            for a in "MBA":
                link(pool.memset(qp[a][:], 0.0))
                link(pool.memset(kp[a][:], 0.0))
                link(pool.memset(kp[a][SHIFT:SHIFT + 2, :, :], -1.0))
                link(pool.memset(vv[a][:], 0.0))
                link(pool.memset(vv[a][:, :, :, HD:HD + 1], 1.0))
            pool.wait_ge(setup_dve, 3)
            pool.wait_ge(ld_w, 16 * 9)
            pool.memset(seen[:], 0.0).then_inc(setup_pool, 1)

            def chain(b, name, k, ins):
                ins.then_inc(sig[name], 1)
                value = in_register(pool, b, name, k)
                pool.wait_ge(setup_pool, 1)
                pool.wait_ge(sig[name], value)

            def power(dst, src):
                return pool.tensor_tensor(dst, src, half_neg[:], ALU.pow)

            def x_norm(b):
                value = in_register(pool, b, "x_stats")
                pool.wait_ge(setup_pool, 1)
                pool.wait_ge(sig["x_stats"], value)
                if not b.first:
                    value = in_register(pool, b.prev, "xr_ready")
                    pool.wait_ge(setup_pool, 1)
                    pool.wait_ge(sig["xr_ready"], value)
                var = mv[:, 0, :, 1]
                chain(b, "x_rstd", 1, pool.tensor_scalar(sq[:, 0, :], var, 1.0, 1e-5, ALU.mult, ALU.add))
                chain(b, "x_rstd", 2, power(sq[:, 1, :], sq[:, 0, :]))
                chain(b, "x_rstd", 3, pool.tensor_tensor(sq[:, 2, :], var, sq[:, 1, :], ALU.mult))
                chain(b, "x_rstd", 4, pool.tensor_tensor(sq[:, 3, :], sq[:, 2, :], sq[:, 1, :], ALU.mult))
                chain(b, "x_rstd", 5, pool.tensor_scalar(sq[:, 4, :], sq[:, 3, :], 1.0, 1e-6, ALU.mult, ALU.add))
                chain(b, "x_rstd", 6, power(sq[:, 5, :], sq[:, 4, :]))
                pool.tensor_scalar(sq[:, 6, :], sq[:, 5, :], 1.0, 0.0, ALU.mult, ALU.add).then_inc(sig["x_rstd"], 1)
                if not b.first:
                    value = in_register(pool, b.prev, "acc_base", 1)
                    pool.wait_ge(setup_pool, 1)
                    pool.wait_ge(sig["acc_base"], value)
                pool.tensor_tensor(res0[:], xs[:], rowv("a_bo").unsqueeze(1).broadcast_to([P, TILES, D]),
                                          ALU.add).then_inc(sig["res0_ready"], 1)

            def m_lat(b):
                value = in_register(pool, b, "lat_stats")
                pool.wait_ge(setup_pool, 1)
                pool.wait_ge(sig["lat_stats"], value)
                if not b.first:
                    value = in_register(pool, b.prev, "latn_ready")
                    pool.wait_ge(setup_pool, 1)
                    pool.wait_ge(sig["latn_ready"], value)
                chain(b, "lat_rstd", 1, pool.tensor_scalar(lsq[:, 0, :], lmv[:, :, 1], 1.0, 1e-5, ALU.mult, ALU.add))
                power(lsq[:, 1, :], lsq[:, 0, :]).then_inc(sig["lat_rstd"], 1)

            def rotated(b, s, k):
                value = in_register(pool, b, "rope_dve", k)
                pool.wait_ge(setup_pool, 1)
                pool.wait_ge(sig["rope_dve"], value)
                f = full[s[1]]
                pool.tensor_tensor(f[:], f[:], rope_s[:], ALU.add).then_inc(sig[f"{s}_full"], 1)

            def split(b, s):
                n = P if s[1] == "q" else kh[s[0].upper()] * HD
                f, r, p = full[s[1]][0:n, :], rest[0:n, :], parts[s[1]]
                value = in_register(pool, b, f"{s}_full")
                pool.wait_ge(setup_pool, 1)
                pool.wait_ge(sig[f"{s}_full"], value)
                for s_last, value in last_user(b, turn_parts, s[1], f"{s}_stored", 16, pool):
                    pool.wait_ge(setup_pool, 1)
                    pool.wait_ge(s_last, value)
                chain(b, f"{s}_split", 1, pool.tensor_scalar(p[0:n, 0, :], f, 1.0, 0.0, ALU.mult, ALU.add))
                chain(b, f"{s}_split", 2, pool.tensor_tensor(r, f, p[0:n, 0, :], ALU.subtract))
                chain(b, f"{s}_split", 3, pool.tensor_scalar(p[0:n, 1, :], r, 1.0, 0.0, ALU.mult, ALU.add))
                chain(b, f"{s}_split", 4, pool.tensor_tensor(p[0:n, 2, :], r, p[0:n, 1, :], ALU.subtract))

            def shift_split(b, a, g):
                value = in_register(pool, b, f"{a}_s1_read", 16 * (g + 1))
                pool.wait_ge(setup_pool, 1)
                pool.wait_ge(sig[f"{a}_s1_read"], value)
                for s_last, value in last_user(b, turn_nms, g % 2, f"{a}_nmT_ps", g + 1, pool):
                    pool.wait_ge(setup_pool, 1)
                    pool.wait_ge(s_last, value)
                chain(b, f"{a}_nms", 2 * g + 1,
                      pool.tensor_scalar(nms[:, g % 2, 0, :], mx[:, g % 2, :], 1.0, 0.0, ALU.mult, ALU.add))
                pool.tensor_tensor(nms[:, g % 2, 1, :], mx[:, g % 2, :], nms[:, g % 2, 0, :], ALU.subtract).then_inc(sig[f"{a}_nms"], 1)

            def score_exp(b, a, g, u):
                if a != "M":
                    return
                n = UNITS2[a] * g + u
                value = in_register(pool, b, "M_exp", n + 1)
                pool.wait_ge(setup_pool, 1)
                pool.wait_ge(sig["M_exp"], value)
                p = probs[:, SLOT[a, g, u], :]
                r = u % 5
                if r in (0, 2):
                    v, pattern = p[:, 0:P], [[1, P]]
                elif r in (1, 3):
                    v, pattern = p.rearrange("p (n q) -> p n q", q=P)[:, 0:4:3, :], [[0, 2], [1, P]]
                else:
                    v, pattern = p.rearrange("p (n q) -> p n q", q=P)[:, 0:4:2, :], [[0, 2], [1, P]]
                pool.affine_select(out=v, in_=v, compare_op=ALU.is_ge, fill=0.0, base=0, pattern=pattern,
                                          channel_multiplier=-1).then_inc(sig["M_masked"], 1)

            def x2_norm(b):
                value = in_register(pool, b, "x2_ready")
                pool.wait_ge(setup_pool, 1)
                pool.wait_ge(sig["x2_ready"], value)
                value = in_register(pool, b, "res0_ready")
                pool.wait_ge(setup_pool, 1)
                pool.wait_ge(sig["res0_ready"], value)
                if not b.first:
                    value = in_register(pool, b.prev, "x1n_ready")
                    pool.wait_ge(setup_pool, 1)
                    pool.wait_ge(sig["x1n_ready"], value)
                pool.tensor_tensor(acc[:], x2[:], res0[:], ALU.add).then_inc(sig["acc_base"], 1)
                value = in_register(pool, b, "x2_stats")
                pool.wait_ge(setup_pool, 1)
                pool.wait_ge(sig["x2_stats"], value)
                if not b.first:
                    value = in_register(pool, b.prev, "r2_ready")
                    pool.wait_ge(setup_pool, 1)
                    pool.wait_ge(sig["r2_ready"], value)
                mean, var = mv[:, 1, :, 0], mv[:, 1, :, 1]
                chain(b, "x2_rstd", 1, pool.tensor_tensor(sq2[:, 0, :], mean, mean, ALU.mult))
                chain(b, "x2_rstd", 2, pool.tensor_tensor(sq2[:, 1, :], sq2[:, 0, :], var, ALU.add))
                chain(b, "x2_rstd", 3, pool.tensor_scalar(sq2[:, 2, :], sq2[:, 1, :], 1.0, 1e-6, ALU.mult, ALU.add))
                power(sq2[:, 3, :], sq2[:, 2, :]).then_inc(sig["x2_rstd"], 1)

            def gate(b):
                value = in_register(pool, b, "ties")
                pool.wait_ge(setup_pool, 1)
                pool.wait_ge(sig["ties"], value)
                if not b.first:
                    value = in_register(pool, b.prev, "acc_dve")
                    pool.wait_ge(setup_pool, 1)
                    pool.wait_ge(sig["acc_dve"], value)
                e = [eq[:, :, n] for n in range(EXPERTS)]
                o = [oneh[:, :, n] for n in range(EXPERTS)]
                chain(b, "one_hot", 1, pool.tensor_scalar(o[0], e[0], 1.0, 0.0, ALU.mult, ALU.add))
                chain(b, "one_hot", 2, pool.tensor_scalar(seen[:, 0, :], e[0], -1.0, 1.0, ALU.mult, ALU.add))
                chain(b, "one_hot", 3, pool.tensor_tensor(o[1], e[1], seen[:, 0, :], ALU.mult))
                chain(b, "one_hot", 4, pool.tensor_tensor(seen[:, 1, :], seen[:, 0, :], o[1], ALU.subtract))
                chain(b, "one_hot", 5, pool.tensor_tensor(o[2], e[2], seen[:, 1, :], ALU.mult))
                chain(b, "one_hot", 6, pool.tensor_tensor(seen[:, 0, :], seen[:, 1, :], o[2], ALU.subtract))
                chain(b, "one_hot", 7, pool.tensor_tensor(o[3], e[3], seen[:, 0, :], ALU.mult))

            def add_b2(b, n):
                if n == 0:
                    value = in_register(pool, b, "gqa_added")
                    pool.wait_ge(setup_pool, 1)
                    pool.wait_ge(sig["gqa_added"], value)
                picked = four(rest[:])
                b2 = rowv("b2")[:, D * n:D * n + D].unsqueeze(1).broadcast_to([P, TILES, D])
                chain(b, "b2_term", n + 1, pool.tensor_tensor(picked, b2, spread(oneh[:, :, n], D), ALU.mult))
                chain(b, "acc_base", n + 2, pool.tensor_tensor(acc[:], acc[:], picked, ALU.add))

            def x1_norm(b):
                value = in_register(pool, b, "x1_stats")
                pool.wait_ge(setup_pool, 1)
                pool.wait_ge(sig["x1_stats"], value)
                if not b.first:
                    value = in_register(pool, b.prev, "x1n_ready")
                    pool.wait_ge(setup_pool, 1)
                    pool.wait_ge(sig["x1n_ready"], value)
                chain(b, "x1_rstd", 1, pool.tensor_scalar(sq1[:, 0, :], l1mv[:, :, 1], 1.0, 1e-5, ALU.mult, ALU.add))
                power(sq1[:, 1, :], sq1[:, 0, :]).then_inc(sig["x1_rstd"], 1)
                if not b.first:
                    value = in_register(pool, b.prev, "y_stored")
                    pool.wait_ge(setup_pool, 1)
                    pool.wait_ge(sig["y_stored"], value)
                pool.tensor_tensor(res1[:], acc[:], rowv("b_bo").unsqueeze(1).broadcast_to([P, TILES, D]),
                                          ALU.add).then_inc(sig["res1_ready"], 1)

            walk(pool, dict(x_norm=x_norm, m_lat=m_lat, m_q=lambda b: rotated(b, "mq", 2),
                            m_k=lambda b: rotated(b, "mk", 4), split=split, shift_split=shift_split,
                            score_exp=score_exp, x2_norm=x2_norm, gate=gate, add_b2=add_b2,
                            x1_norm=x1_norm), [turn_nms, turn_parts])


def kernel(**inputs):
    import concourse.bacc as bacc
    from concourse.bass_utils import run_bass_kernel_spmd

    a = {n: np.asarray(v) for n, v in inputs.items()}
    swap = np.arange(D) ^ (HD // 2)

    def attn(n):
        return a["L0_attn_" + n]

    def ffn(n):
        return a["L0_ffn_" + n]

    def l1(n):
        return a["L1_attn_" + n]

    cols = {"a_wq": attn("wq").T, "a_wk": attn("wk").T, "a_wv": attn("wv").T,
            "a_wo": attn("wo").T,
            "m_wq": ffn("Wq").T, "m_wqs": ffn("Wq").T[:, swap], "m_wdkv": ffn("Wdkv").T, "m_wo": ffn("Wo").T,
            "gate": ffn("gate_w").T, "b_wq": l1("Wq"), "b_wk": l1("Wk"), "b_wv": l1("Wv"), "b_wo": l1("Wo")}
    w_all = np.concatenate([cols[n] for n in WCOLS], axis=1)
    w_lat = np.zeros((P, 384), np.float32)
    w_lat[:LATENT] = np.concatenate([ffn("Wuk").T, ffn("Wuk").T[:, swap], ffn("Wuv").T], axis=1)
    v_all = np.zeros((P, VN), np.float32)
    for n, src in (("a_bq", attn("bq")), ("a_bk", attn("bk")), ("norm1", ffn("norm1_w")), ("norm2", ffn("norm2_w")),
                   ("ln_g", ffn("ln_g")), ("ln_b", ffn("ln_b")), ("b_bq", l1("bq")), ("b_bk", l1("bk"))):
        v_all[:len(src), VCOLS[n]] = src
    v_all[:, VCOLS["b1"]:] = ffn("b1").reshape(EXPERTS * HCH, P).T
    rows = {"a_bv": attn("bv"), "a_bo": attn("bo"), "gate_b": ffn("gate_b"), "b2": ffn("b2").reshape(-1),
            "b_bv": l1("bv"), "b_bo": l1("bo")}
    r_all = np.concatenate([rows[n] for n in RCOLS])
    w1 = ffn("W1").transpose(2, 0, 1).reshape(D, EXPERTS * HIDDEN)
    w2 = ffn("W2").transpose(2, 0, 1).reshape(HCH, P, EXPERTS, D).transpose(1, 2, 0, 3)
    wi_up = np.concatenate([a["L1_ffn_w_gate"].T, a["L1_ffn_w_up"].T], axis=1)
    wi_down = a["L1_ffn_w_down"].T.reshape(FCH, P, D).transpose(1, 0, 2).reshape(P, FF1)

    half = HD // 2
    inv_freq = (1.0 / 10000.0 ** (np.arange(half, dtype=np.float32) / half)).astype(np.float32)
    angle = np.arange(SEQ, dtype=np.float32)[:, None] * inv_freq[None, :]
    ch = np.arange(D) % HD
    cos, sin = np.cos(angle).T[ch % half], np.sin(angle).T[ch % half]
    sin = sin * np.where(ch < half, -1.0, 1.0)[:, None]
    rope = np.stack([cos, sin], axis=1).astype(np.float32)

    nc = bacc.Bacc("TRN2", target_bir_lowering=False, num_devices=1)
    arrays, args = {}, []
    for name, arr in (("x", attn("x")), ("w_all", w_all), ("w_lat", w_lat), ("v_all", v_all), ("r_all", r_all),
                      ("w1", w1), ("w2", w2), ("wi_up", wi_up), ("wi_down", wi_down), ("rope", rope)):
        arr = np.ascontiguousarray(arr)
        arrays[name] = arr
        args.append(nc.dram_tensor(name, arr.shape, mybir.dt.from_np(arr.dtype), kind="ExternalInput").ap())
    args.append(nc.dram_tensor("out", (BATCH, SEQ, D), F32, kind="ExternalOutput").ap())
    kernel_program(nc, *args)
    r = run_bass_kernel_spmd(nc, [arrays], core_ids=[0])
    return r.results[0]["out"]
```

```python
from contextlib import ExitStack

import numpy as np
import concourse.bass as bass
from concourse import mybir

F32 = mybir.dt.float32
BF16 = mybir.dt.bfloat16
I32 = mybir.dt.int32
ALU = mybir.AluOpType
ACT = mybir.ActivationFunctionType
AX = mybir.AxisListType

P = 128
BATCH, SEQ, D = 16, 512, 128
TILES = SEQ // P
HEADS, HD = 16, 8
GROUP = 4
GROUPS = HEADS // GROUP
VW = 32
KV0 = 4
LATENT = 64
EXPERTS, HIDDEN = 4, 512
HCH = HIDDEN // P
FF1 = 384
FCH = FF1 // P
SCALE = float(HD) ** -0.5
PARTS = 3
PROD = PARTS * PARTS * HD
ROWS1 = 96
SHIFT = 96
ROWS2 = 98
LOWEST = -3.0e38
MASKED = -1.0e30

WCOLS = {}
_at = 0
for _n, _w in (("a_wq", 128), ("a_wk", 32), ("a_wv", 32), ("a_wo", 128),
               ("m_wq", 128), ("m_wqs", 128), ("m_wdkv", LATENT), ("m_wo", 128), ("gate", EXPERTS),
               ("b_wq", 128), ("b_wk", HD), ("b_wv", HD), ("b_wo", 128)):
    WCOLS[_n] = (_at, _at + _w)
    _at += _w
WN = _at
VCOLS = {n: i for i, n in enumerate(("a_bq", "a_bk", "norm1", "norm2", "ln_g", "ln_b", "b_bq", "b_bk", "b1"))}
VN = len(VCOLS) - 1 + EXPERTS * HCH
RCOLS = {}
_at = 0
for _n, _w in (("a_bv", 32), ("a_bo", 128), ("gate_b", EXPERTS), ("b2", EXPERTS * D), ("b_bv", HD), ("b_bo", 128)):
    RCOLS[_n] = (_at, _at + _w)
    _at += _w
RN = _at

PERIOD = 12
START = {"M": 3.0, "A": 7.0, "B": 23.0}
NS1, NPV = 3, 1
LEAD = 1.0
LAG = 1.936
CAUSAL_UNITS = 10
UNITS2 = {"M": CAUSAL_UNITS, "A": 16, "B": 16}


def stages():
    out = []

    def put(t, name, *args):
        out.append((t + LEAD, len(out), name, args))

    put(-0.9, "x_load")
    put(0.0, "x_norm")
    put(0.617, "x_scaled")
    put(0.9, "turn", "xr")
    put(1.12, "m_q")
    put(1.25, "split", "mq")
    put(1.8, "pack", "mq")
    put(0.98, "m_lat")
    put(1.55, "m_lat_turn")
    put(1.7, "m_k")
    put(1.85, "split", "mk")
    put(2.4, "pack", "mk")
    put(1.95, "m_v")
    put(2.15, "turn", "xn")
    put(2.55, "a_q")
    put(2.7, "split", "aq")
    put(3.25, "pack", "aq")
    put(2.83, "a_k")
    put(3.523, "split", "ak")
    put(4.073, "pack", "ak")
    put(3.472, "a_v")
    for a in "MAB":
        s = START[a]
        for g in range(GROUPS):
            for u in range(16):
                put(s + g + u / 16, "score_max", a, g, u)
            put(s + g + 1.15, "shift_split", a, g)
            put(s + g + 1.45, "shift_turn", a, g)
            n = UNITS2[a]
            for u in range(n):
                put(s + LAG + g + (u + 0.5) / n, "score_exp", a, g, u)
                late = (3.5 if a == "M" else 2.7) * n / 16 + 2.3 * n / 16 * (1 - u / (n - 1))
                put(s + LAG + g + (u + 0.5 + late) / n, "probs_v", a, g, u)
            e = s + LAG + g + 1.188
            put(e, "out_copy", a, g)
            put(e + 0.183, "out_turn", a, g)
    for a in "MAB":
        e = START[a] + LAG + 3 + 1.188 + 0.183 + 0.149
        put(e, "o_turn", a)
        put(e + 0.382, "o_proj", a)
        if a == "M":
            put(e + 0.382 + 0.352, "x2_norm")
    e0 = 14.852
    put(e0 - 0.628, "x2_scaled")
    put(e0 - 0.5, "turn", "r2")
    put(e0 - 0.174, "gate")
    step = 0.133
    t = e0
    for e in range(EXPERTS):
        for c in range(HCH):
            put(t, "up", e, c)
            t += step
            if e and c in (1, 3):
                put(t - step * 0.5, "down", e - 1, c // 2)
                t += step
    put(t + 0.1, "down", EXPERTS - 1, 0)
    put(t + 0.2, "down", EXPERTS - 1, 1)
    for e in range(EXPERTS):
        put(e0 + 0.15 * e, "add_b2", e)
    b0 = t + 0.3
    put(b0, "x1_norm")
    put(b0 + 0.121, "x1_scaled")
    put(b0 + 0.6, "turn", "x1")
    put(b0 + 0.8, "b_q")
    put(b0 + 0.8 + 0.1, "split", "bq")
    put(b0 + 0.8 + 0.1 + 0.55, "pack", "bq")
    put(b0 + 1.0, "b_k")
    put(b0 + 1.0 + 0.1, "split", "bk")
    put(b0 + 1.0 + 0.1 + 0.55, "pack", "bk")
    put(b0 + 1.19, "b_v")
    f0 = b0 + 1.0
    for c in range(FCH):
        put(f0 + 0.02 * c, "ff_up", c)
    put(f0 + 0.02 * 2 + 0.465, "ff_down")
    return out


def ordered(late={}):
    rows = ((t + late.get(name, 0.0), order, name, args) for t, order, name, args in stages())
    return sorted((t % PERIOD, order, name, args, int(t // PERIOD)) for t, order, name, args in rows)


def spare_users(name, *args):
    a, g = (args + (None, None))[:2]
    return {
        "turn": [(f"{a}_T", 1)], "m_q": [("rope_dve", 1), ("rope_dve", 2)], "m_lat": [("lat_copied", 1)],
        "m_lat_turn": [("latT_ready", 1)], "m_k": [("rope_dve", 3), ("rope_dve", 4)], "m_v": [("mv_ready", 1)],
        "a_q": [("aq_full", 1)], "a_k": [("ak_full", 1)], "a_v": [("av_ready", 1)],
        "b_q": [("bq_full", 1)], "b_k": [("bk_full", 1)], "b_v": [("bv_ready", 1)],
        "shift_turn": [(f"{a}_nmT", g + 1)] if name == "shift_turn" else [],
        "out_turn": [(f"{a}_otok", g + 1)] if name == "out_turn" else [],
        "o_turn": [(f"{a}_oT", 1)], "o_proj": [({"M": "x2_ready", "A": "gqa_added", "B": "y_ready"}.get(a), 1)],
        "gate": [("logits", 1)],
        "up": [("hid_act" if (HCH * a + g) % 2 else "hid_dve", (HCH * a + g) // 2 + 1)]
              if name == "up" else [],
        "down": [("acc_dve", 2 * a + g + 1)] if name == "down" else [],
        "ff_up": [("ff_gate", a + 1), ("ff_hid", a + 1)] if name == "ff_up" else [],
        "ff_down": [("res_b", 1)],
    }.get(name, [])


LAST = 2


def kernel_program(nc, x, w_all, w_lat, v_all, r_all, w1, w2, wi_up, wi_down, rope, out):
    table = ordered()
    assert max(row[4] for row in table) == LAST

    q_parts = {a: nc.dram_tensor(f"q_parts_{a}", (PARTS, D, SEQ), BF16).ap() for a in "MBA"}
    kh = {"M": HEADS, "A": KV0, "B": 1}
    k_parts = {a: nc.dram_tensor(f"k_parts_{a}", (PARTS, kh[a] * HD, SEQ), BF16).ap() for a in "MBA"}

    nc.disable_value_cache = True
    ctx = ExitStack()
    with ctx:
        def sb(name, shape, dt=F32):
            return ctx.enter_context(nc.sbuf_tensor(name, shape, dt))

        def pb(name):
            return ctx.enter_context(nc.psum_tensor(name, [P, 512], F32))

        def sem(name):
            return ctx.enter_context(nc.semaphore(name))

        w = sb("w", [P, WN])
        wl = sb("wl", [P, 384])
        vec = sb("vec", [P, VN])
        row = sb("row", [P, RN])
        w1s = sb("w1s", [P, EXPERTS * HIDDEN])
        w2s = sb("w2s", [P, EXPERTS, HCH, D])
        wgu = sb("wgu", [P, 2 * FF1])
        wd = sb("wd", [P, FCH, D])
        rot = sb("rot", [P, 2, SEQ])
        ident = sb("ident", [P, P])
        identb = sb("identb", [P, P], BF16)
        mask = sb("mask", [P, SEQ])
        half_neg = sb("half_neg", [P, TILES])

        xs = sb("xs", [P, TILES, D])
        bn = sb("bn", [P, 2, TILES, 6])
        mv = sb("mv", [P, 2, TILES, 2])
        sq = sb("sq", [P, 7, TILES])
        sq2 = sb("sq2", [P, 4, TILES])
        sq1 = sb("sq1", [P, 2, TILES])
        xn = sb("xn", [P, TILES, D])
        factored = sb("factored", [P, TILES, D])
        xnT = sb("xnT", [P, SEQ])
        xrT = sb("xrT", [P, SEQ])
        res0 = sb("res0", [P, TILES, D])
        x2 = sb("x2", [P, TILES, D])
        r2T = sb("r2T", [P, SEQ])
        acc = sb("acc", [P, TILES, D])
        x1T = sb("x1T", [P, SEQ])
        res1 = sb("res1", [P, TILES, D])
        lat = sb("lat", [P, TILES, LATENT])
        latn = sb("latn", [P, TILES, LATENT])
        latT = sb("latT", [P, SEQ])
        lbn = sb("lbn", [P, TILES, 6])
        lmv = sb("lmv", [P, TILES, 2])
        lsq = sb("lsq", [P, 2, TILES])
        rope_s = sb("rope_s", [P, SEQ])
        full = {s: sb(f"full_{s}", [P, SEQ]) for s in "qk"}
        rest = sb("rest", [P, SEQ])
        parts = {s: sb(f"parts_{s}", [P, PARTS, SEQ], BF16) for s in "qk"}
        qp = {a: sb(f"qp_{a}", [P, HEADS, SEQ], BF16) for a in "MBA"}
        kp = {a: sb(f"kp_{a}", [P, kh[a], SEQ], BF16) for a in "MBA"}
        vv = {a: sb(f"vv_{a}", [P, TILES, kh[a], VW]) for a in "MBA"}
        mx = sb("mx", [P, 2, 16])
        minus = sb("minus", [2, SEQ], BF16)
        nms = sb("nms", [P, 2, 2, 16], BF16)
        nmT = sb("nmT", [32, 2, P], BF16)
        NPR = 6
        probs = sb("probs", [P, NPR, SEQ])
        osb = sb("osb", [P, 2, SEQ])
        rc = sb("rc", [P, 2, 16])
        otok = sb("otok", [P, TILES, D])
        oT = sb("oT", [P, SEQ])
        lg = sb("lg", [P, TILES, EXPERTS])
        lmax = sb("lmax", [P, TILES])
        l1bn = sb("l1bn", [P, TILES, 6])
        l1mv = sb("l1mv", [P, TILES, 2])
        eq = sb("eq", [P, TILES, EXPERTS])
        seen = sb("seen", [P, 2, TILES])
        oneh = sb("oneh", [P, TILES, EXPERTS])
        NH = 8
        hid = sb("hid", [P, NH, SEQ])
        wi = hid[:, 0:3, :].rearrange("p c n -> p (c n)").bitcast(I32)
        th = sb("th", [P, SEQ])
        hf = sb("hf", [P, FCH, SEQ])

        s1 = [pb(f"s1_{i}") for i in range(NS1)]
        s2 = [pb(f"s2_{i}") for i in range(2)]
        pv = [pb(f"pv_{i}") for i in range(NPV)]
        misc = [pb(f"misc_{i}") for i in range(2)]

        sig, PER = {}, {}

        def declare(name, per):
            sig[name], PER[name] = sem(name), per

        ld_w, ld_moe, ld_int, cleared, setup_dve, setup_pool, pool_chain = (
            sem(n) for n in ("ld_w", "ld_moe", "ld_int", "cleared", "setup_dve", "setup_pool", "pool_chain"))
        for name, per in (
                ("x_loaded", 16), ("x_bn", 1), ("x_stats", 1), ("x_rstd", 7), ("xn_ready", 1), ("xr_ready", 1),
                ("res0_ready", 1), ("turned_xr", 1), ("turned_xn", 1), ("turned_r2", 1), ("turned_x1", 1),
                ("xr_T", 1), ("xn_T", 1), ("r2_T", 1), ("x1_T", 1),
                ("mq_ps", 2), ("mk_ps", 2), ("rope_dve", 4), ("mq_full", 1), ("mk_full", 1),
                ("lat_ps", 1), ("lat_copied", 1), ("lat_bn", 1), ("lat_stats", 1), ("lat_rstd", 2),
                ("latn_ready", 1), ("latT_ps", 1), ("latT_ready", 1), ("mv_ps", 1), ("mv_ready", 1),
                ("a_ps", 3), ("aq_full", 1), ("ak_full", 1), ("av_ready", 1),
                ("b_ps", 3), ("bq_full", 1), ("bk_full", 1), ("bv_ready", 1),
                ("x2_ready", 1), ("x2_bn", 1), ("x2_stats", 1), ("x2_rstd", 4), ("r2_ready", 1),
                ("gate_ps", 1), ("logits", 1), ("top", 1), ("ties", 1), ("one_hot", 7), ("acc_base", 1 + EXPERTS),
                ("b2_term", EXPERTS),
                ("up_ps", 16), ("hid_act", 8), ("hid_dve", 8), ("down_ps", 8), ("acc_dve", 8),
                ("gqa_added", 1), ("x1_bn", 1), ("x1_stats", 1), ("x1_rstd", 2), ("x1n_ready", 1), ("res1_ready", 1),
                ("ff_ps", 2 * FCH), ("tanh_done", FCH), ("ff_gate", FCH), ("ff_hid", FCH), ("ffd_ps", 1),
                ("res_b", 1),
                ("y_ready", 1), ("y_stored", 16)):
            declare(name, per)
        for s in ("mq", "mk", "aq", "ak", "bq", "bk"):
            declare(f"{s}_split", 4)
            declare(f"{s}_stored", 16)
            declare(f"{s}_packed", 16 * (PARTS * PARTS))
        for a in "MBA":
            declare(f"{a}_s1_ps", 64)
            declare(f"{a}_s1_read", 64)
            declare(f"{a}_nms", 2 * GROUPS)
            declare(f"{a}_nmT_ps", GROUPS)
            declare(f"{a}_nmT", GROUPS)
            declare(f"{a}_shift", 32 * GROUPS)
            declare(f"{a}_s2_ps", GROUPS * UNITS2[a])
            declare(f"{a}_exp", GROUPS * UNITS2[a])
            declare(f"{a}_pv", GROUPS * UNITS2[a])
            declare(f"{a}_osb", GROUPS)
            declare(f"{a}_ot_ps", GROUPS)
            declare(f"{a}_rc", GROUPS)
            declare(f"{a}_otok", GROUPS)
            declare(f"{a}_oT_ps", 1)
            declare(f"{a}_oT", 1)
            declare(f"{a}_o_ps", 1)
        declare("M_masked", GROUPS * CAUSAL_UNITS)

        class At:

            def __init__(self, i, o, times=None):
                self.i, self.o, self.times = i, o, times
                self.first = isinstance(i, int) and i == o

            @property
            def prev(self):
                return At(self.i, self.o + 1, self.times)

        def total(b, name, k=None):
            per = PER[name]
            k = per if k is None else k
            return (b.i - b.o) * per + k if isinstance(b.i, int) else b.times[per] + (k - b.o * per)

        names = [0]

        def in_register(eng, b, name, k=None):
            if isinstance(b.i, int):
                return total(b, name, k)
            per = PER[name]
            names[0] += 1
            with eng.register(f"value_{names[0]}") as value:
                eng.reg_add(value, b.times[per], (per if k is None else k) - b.o * per)
            return value

        def last_user(b, turn, key, name, k, eng=None):
            was = turn.get(key)
            turn[key] = (name, k, b.o)
            if was is None:
                return []
            n, kk, o = was
            at = At(b.i, o, b.times)
            return [(sig[n], total(at, n, kk) if eng is None else in_register(eng, at, n, kk))]

        def walk(eng, steps, turns, table=table):
            def iteration(i, times=None):
                for t in turns:
                    for key in t:
                        n, k, o = t[key]
                        t[key] = (n, k, o + 1)
                for _, _, name, args, o in table:
                    if name in steps and not (isinstance(i, int) and not 0 <= i - o < BATCH):
                        steps[name](At(i, o, times), *args)
            for i in range(LAST + 1):
                iteration(i)
            before = [dict(t) for t in turns]
            with eng.Fori(LAST + 1, BATCH) as i:
                times = {}
                with ExitStack() as held:
                    for per in sorted(set(PER.values())):
                        count = held.enter_context(eng.register(f"times_{per}_{eng.engine.name}"))
                        eng.reg_mul(count, i, per)
                        times[per] = eng.snap(count, donate=True, min_val=(LAST + 1) * per, max_val=BATCH * per)
                    iteration(i, times)
            assert before == [dict(t) for t in turns]
            for i in range(BATCH, BATCH + LAST):
                iteration(i)

        SPARE, SLOT, BANK = {}, {}, {}
        for _, _, name, args, _ in table:
            for key in spare_users(name, *args):
                SPARE[key] = len(SPARE) % 2
            if name == "score_max":
                BANK[args] = len(BANK) % NS1
            if name == "score_exp":
                SLOT[args] = len(SLOT) % NPR

        block = ctx.enter_context(nc.Block())

        def wc(name):
            return w[:, WCOLS[name][0]:WCOLS[name][1]]

        def rowv(name):
            return row[:, RCOLS[name][0]:RCOLS[name][1]]

        def vcol(name, n=P, k=0):
            return vec[0:n, VCOLS[name] + k:VCOLS[name] + k + 1]

        def spread(ap, n):
            return ap.unsqueeze(2).broadcast_to([ap.shape[0], ap.shape[1], n])

        def four(ap):
            return ap.rearrange("p (t d) -> p t d", t=TILES)

        def causal_parts(u):
            pair, r = divmod(u, 5)
            h0, h1 = 2 * pair, 2 * pair + 1
            if r in (0, 2):
                return [((h0, h1)[r // 2], 0, 0, 512)]
            if r in (1, 3):
                return [((h0, h1)[r // 2], 1, 0, 384), ((h0, h1)[r // 2], 3, 384, 128)]
            return [(h0, 2, 0, 256), (h1, 2, 256, 256)]

        def unit_parts(a, u):
            return causal_parts(u) if a == "M" else [(u // TILES, u % TILES, 0, SEQ)]

        def last_in_head(a, u, c):
            return c == (2 if a == "M" else TILES - 1)

        KHEAD = {"M": lambda h: h, "A": lambda h: h // (HEADS // KV0), "B": lambda h: 0}

        @block.sync
        def _(sp):
            for dst, src in ((w, w_all), (wl, w_lat), (vec, v_all), (rot, rope)):
                sp.dma_start(dst[:], src).then_inc(ld_w, 16)
            sp.dma_start(row[:], r_all.partition_broadcast(P)).then_inc(ld_w, 16)

            def load_rest():
                sp.wait_ge(setup_pool, 1)
                zeros = mask[0:ROWS1 - PROD, 0:SEQ // 2].bitcast(BF16).unsqueeze(1)
                for a in "MAB":
                    for dst, src, n in ((qp[a][PROD:ROWS1], zeros, HEADS), (kp[a][PROD:ROWS1], zeros, kh[a]),
                                        (kp[a][SHIFT:ROWS2], minus[:].unsqueeze(1), kh[a])):
                        sp.dma_start(dst, src.broadcast_to([dst.shape[0], n, SEQ])).then_inc(cleared, 16)
                for dst, src in ((w1s, w1), (w2s, w2)):
                    sp.dma_start(dst[:], src).then_inc(ld_moe, 16)
                sp.dma_start(wi[:, 0:2 * FF1], wi_up).then_inc(ld_int, 16)
                sp.dma_start(wi[:, 2 * FF1:3 * FF1], wi_down).then_inc(ld_int, 16)

            def batch(ap, b):
                i = b.i if not b.o else b.i - b.o
                if isinstance(i, int):
                    return ap[i].rearrange("(t p) d -> p t d", p=P)
                return ap[bass.ds(i, 1)].rearrange("a (t p) d -> p (a t) d", p=P)

            def x_load(b):
                if not b.first:
                    value = in_register(sp, b.prev, "xn_ready")
                    sp.wait_ge(setup_pool, 1)
                    sp.wait_ge(sig["xn_ready"], value)
                if not b.first:
                    value = in_register(sp, b.prev, "res0_ready")
                    sp.wait_ge(setup_pool, 1)
                    sp.wait_ge(sig["res0_ready"], value)
                sp.dma_start(xs[:], batch(x, b)).then_inc(sig["x_loaded"], 16)
                if b.first:
                    load_rest()

            def shift_turn(b, a, g):
                value = in_register(sp, b, f"{a}_nmT", g + 1)
                sp.wait_ge(setup_pool, 1)
                sp.wait_ge(sig[f"{a}_nmT"], value)
                if g == 0:
                    if not b.first:
                        value = in_register(sp, b.prev, f"{a}_s2_ps")
                        sp.wait_ge(setup_pool, 1)
                        sp.wait_ge(sig[f"{a}_s2_ps"], value)
                for s in range(2):
                    sp.dma_start(qp[a][SHIFT + s:SHIFT + s + 1, GROUP * g:GROUP * g + GROUP, :],
                                        nmT[16 * s:16 * s + 16, g % 2, :]).then_inc(sig[f"{a}_shift"], 16)

            def split(b, s):
                a, is_q = s[0].upper(), s[1] == "q"
                n = HEADS * HD if is_q else kh[a] * HD
                scratch = q_parts[a] if is_q else k_parts[a]
                value = in_register(sp, b, f"{s}_split")
                sp.wait_ge(setup_pool, 1)
                sp.wait_ge(sig[f"{s}_split"], value)
                if not b.first:
                    value = in_register(sp, b.prev, f"{s}_packed")
                    sp.wait_ge(setup_pool, 1)
                    sp.wait_ge(sig[f"{s}_packed"], value)
                sp.dma_start(scratch.rearrange("s c n -> c s n"), parts[s[1]][0:n, :, :]) \
                    .then_inc(sig[f"{s}_stored"], 16)

            def pack(b, s):
                a, is_q = s[0].upper(), s[1] == "q"
                scratch = q_parts[a] if is_q else k_parts[a]
                value = in_register(sp, b, f"{s}_stored")
                sp.wait_ge(setup_pool, 1)
                sp.wait_ge(sig[f"{s}_stored"], value)
                if not b.first:
                    value = in_register(sp, b.prev, f"{a}_s2_ps")
                    sp.wait_ge(setup_pool, 1)
                    sp.wait_ge(sig[f"{a}_s2_ps"], value)
                if not b.first:
                    value = in_register(sp, b.prev, f"{a}_s1_ps")
                    sp.wait_ge(setup_pool, 1)
                    sp.wait_ge(sig[f"{a}_s1_ps"], value)
                if b.first and s == "mq":
                    sp.wait_ge(cleared, 16 * 9)
                for i in range(PARTS):
                    for j in range(PARTS):
                        r = (PARTS * i + j) * HD
                        sp.dma_start((qp if is_q else kp)[a][r:r + HD, :, :],
                                            scratch[i if is_q else j].rearrange("(h d) n -> d h n", d=HD)) \
                                                .then_inc(sig[f"{s}_packed"], 16)

            def o_proj(b, a):
                if a == "B":
                    value = in_register(sp, b, "y_ready")
                    sp.wait_ge(setup_pool, 1)
                    sp.wait_ge(sig["y_ready"], value)
                    sp.dma_start(batch(out, b), res1[:]).then_inc(sig["y_stored"], 16)

            walk(sp, {"x_load": x_load, "shift_turn": shift_turn, "split": split, "pack": pack, "o_proj": o_proj}, [],
                 ordered({"split": 0.3, "shift_turn": 0.03}))
            sp.wait_ge(sig["y_stored"], 16 * BATCH)

        @block.tensor
        def _(pe):
            banks = {}
            pe.wait_ge(ld_w, 16 * 5)
            pe.wait_ge(setup_pool, 1)
            turn_misc, turn_s1, turn_s2, turn_pv = {}, {}, {}, {}

            def misc_bank(b, name, k):
                m = SPARE[name, k]
                for s_last, value in last_user(b, turn_misc, m, name, k):
                    pe.wait_ge(s_last, value)
                return misc[m]

            def turns4(dst, src, name):
                for t in range(TILES):
                    ins = pe.transpose(dst[:, P * t:P * t + P], src[:, t, :], ident[:])
                ins.then_inc(sig[name], 1)

            def turn(b, what):
                src, ready, done = {"xr": (factored, "xr_ready", "xr_T"), "xn": (xn, "xn_ready", "xn_T"),
                                    "r2": (factored, "r2_ready", "r2_T"), "x1": (factored, "x1n_ready", "x1_T")}[what]
                m = misc_bank(b, done, 1)
                pe.wait_ge(sig[ready], total(b, ready))
                turns4(m, src, "turned_" + what)

            def dense(m, n, lhsT, rhs, name):
                pe.matmul(m[0:n, :], lhsT, rhs, start=True, stop=True).then_inc(sig[name], 1)

            def m_q(b):
                pe.wait_ge(sig["xr_T"], total(b, "xr_T"))
                for j, wn in enumerate(("m_wq", "m_wqs")):
                    dense(misc_bank(b, "rope_dve", 1 + j), P, wc(wn), xrT[:], "mq_ps")

            def m_lat(b):
                pe.wait_ge(sig["xr_T"], total(b, "xr_T"))
                m = misc_bank(b, "lat_copied", 1)
                for t in range(TILES):
                    ins = pe.matmul(m[:, LATENT * t:LATENT * t + LATENT], xrT[:, P * t:P * t + P], wc("m_wdkv"),
                                    start=True, stop=True)
                ins.then_inc(sig["lat_ps"], 1)

            def m_lat_turn(b):
                m = misc_bank(b, "latT_ready", 1)
                value = in_register(pe, b, "latn_ready")
                pe.wait_ge(setup_pool, 1)
                pe.wait_ge(sig["latn_ready"], value)
                for t in range(TILES):
                    ins = pe.transpose(m[0:LATENT, P * t:P * t + P], latn[:, t, :], ident[:])
                ins.then_inc(sig["latT_ps"], 1)

            def m_k(b):
                pe.wait_ge(sig["latT_ready"], total(b, "latT_ready"))
                for j in range(2):
                    dense(misc_bank(b, "rope_dve", 3 + j), P, wl[:, P * j:P * j + P], latT[:], "mk_ps")

            def values(b, src, weight, width, done, name):
                m = misc_bank(b, done, 1)
                for t in range(TILES):
                    ins = pe.matmul(m[:, width * t:width * t + width], src[:, P * t:P * t + P], weight,
                                    start=True, stop=True)
                ins.then_inc(sig[name], 1)

            def m_v(b):
                values(b, latT, wl[:, 2 * P:3 * P], P, "mv_ready", "mv_ps")

            def a_q(b):
                pe.wait_ge(sig["xn_T"], total(b, "xn_T"))
                dense(misc_bank(b, "aq_full", 1), P, wc("a_wq"), xnT[:], "a_ps")

            def a_k(b):
                dense(misc_bank(b, "ak_full", 1), KV0 * HD, wc("a_wk"), xnT[:], "a_ps")

            def a_v(b):
                values(b, xnT, wc("a_wv"), KV0 * HD, "av_ready", "a_ps")

            def b_q(b):
                pe.wait_ge(sig["x1_T"], total(b, "x1_T"))
                dense(misc_bank(b, "bq_full", 1), P, wc("b_wq"), x1T[:], "b_ps")

            def b_k(b):
                dense(misc_bank(b, "bk_full", 1), HD, wc("b_wk"), x1T[:], "b_ps")

            def b_v(b):
                values(b, x1T, wc("b_wv"), HD, "bv_ready", "b_ps")

            def score_max(b, a, g, u):
                n = 16 * g + u
                if n == 0:
                    low = a.lower()
                    pe.wait_ge(sig[f"{low}q_packed"], total(b, f"{low}q_packed"))
                    pe.wait_ge(sig[f"{low}k_packed"], total(b, f"{low}k_packed"))
                h, t = GROUP * g + u // TILES, u % TILES
                keys = P * (t + 1) if a == "M" else SEQ
                for s_last, value in last_user(b, turn_s1, BANK[a, g, u], f"{a}_s1_read", n + 1):
                    pe.wait_ge(s_last, value)
                pe.matmul(s1[BANK[a, g, u]][:, 0:keys], qp[a][0:ROWS1, h, P * t:P * t + P],
                                 kp[a][0:ROWS1, KHEAD[a](h), 0:keys], start=True, stop=True) \
                                     .then_inc(sig[f"{a}_s1_ps"], 1)

            def shift_turn(b, a, g):
                m = misc_bank(b, f"{a}_nmT", g + 1)
                pe.wait_ge(sig[f"{a}_nms"], total(b, f"{a}_nms", 2 * g + 2))
                mb = m[:].bitcast(BF16)
                pe.transpose(mb[0:32, 0:P], nms[:, g % 2].rearrange("p s n -> p (s n)"), identb[:]) \
                    .then_inc(sig[f"{a}_nmT_ps"], 1)

            def score_exp(b, a, g, u):
                n = UNITS2[a] * g + u
                if u == 0:
                    pe.wait_ge(sig[f"{a}_shift"], total(b, f"{a}_shift", 32 * (g + 1)))
                for s_last, value in last_user(b, turn_s2, n % 2, f"{a}_exp", n + 1):
                    pe.wait_ge(s_last, value)
                for hh, c, col, q in unit_parts(a, u):
                    h = GROUP * g + hh
                    ins = pe.matmul(s2[n % 2][:, col:col + q], kp[a][0:ROWS2, KHEAD[a](h), P * c:P * c + P],
                                    qp[a][0:ROWS2, h, SEQ - q:SEQ], start=True, stop=True)
                ins.then_inc(sig[f"{a}_s2_ps"], 1)

            def probs_v(b, a, g, u):
                n = UNITS2[a] * g + u
                probabilities = "M_masked" if a == "M" else f"{a}_exp"
                pe.wait_ge(sig[probabilities], total(b, probabilities, n + 1))
                if n == 0:
                    values_in = f"{a.lower()}v_ready"
                    pe.wait_ge(sig[values_in], total(b, values_in))
                if u == 0:
                    for s_last, value in last_user(b, turn_pv, g % NPV, f"{a}_osb", g + 1):
                        pe.wait_ge(s_last, value)
                slot = SLOT[a, g, u]
                for hh, c, col, q in unit_parts(a, u):
                    ins = pe.matmul(pv[g % NPV][32 * hh:32 * hh + VW, SEQ - q:SEQ],
                                    vv[a][:, c, KHEAD[a](GROUP * g + hh), :], probs[:, slot, col:col + q],
                                    start=(c == 0), stop=last_in_head(a, u, c), tile_position=(0, 32 * hh))
                ins.then_inc(sig[f"{a}_pv"], 1)

            def out_turn(b, a, g):
                m = misc_bank(b, f"{a}_otok", g + 1)
                pe.wait_ge(sig[f"{a}_osb"], total(b, f"{a}_osb", g + 1))
                for t in range(TILES):
                    ins = pe.transpose(m[:, P * t:P * t + P], osb[:, g % 2, P * t:P * t + P], ident[:])
                ins.then_inc(sig[f"{a}_ot_ps"], 1)

            def o_turn(b, a):
                m = misc_bank(b, f"{a}_oT", 1)
                pe.wait_ge(sig[f"{a}_otok"], total(b, f"{a}_otok"))
                turns4(m, otok, f"{a}_oT_ps")

            def o_proj(b, a):
                m = misc_bank(b, {"M": "x2_ready", "A": "gqa_added", "B": "y_ready"}[a], 1)
                pe.wait_ge(sig[f"{a}_oT"], total(b, f"{a}_oT"))
                for t in range(TILES):
                    ins = pe.matmul(m[:, P * t:P * t + P], oT[:, P * t:P * t + P], wc(f"{a.lower()}_wo"),
                                    start=True, stop=True)
                ins.then_inc(sig[f"{a}_o_ps"], 1)

            def gate(b):
                m = misc_bank(b, "logits", 1)
                pe.wait_ge(sig["r2_T"], total(b, "r2_T"))
                for t in range(TILES):
                    ins = pe.matmul(m[:, EXPERTS * t:EXPERTS * t + EXPERTS], r2T[:, P * t:P * t + P], wc("gate"),
                                    start=True, stop=True)
                ins.then_inc(sig["gate_ps"], 1)

            def up(b, e, c):
                n = HCH * e + c
                if b.first and n == 0:
                    pe.wait_ge(ld_moe, 16 * 2)
                m = misc_bank(b, "hid_act" if n % 2 else "hid_dve", n // 2 + 1)
                pe.matmul(m[:], w1s[:, P * n:P * n + P], r2T[:], start=True, stop=True).then_inc(sig["up_ps"], 1)

            def down(b, e, half):
                m = misc_bank(b, "acc_dve", 2 * e + half + 1)
                pe.wait_ge(sig["hid_act"], total(b, "hid_act", 2 * e + 2))
                pe.wait_ge(sig["hid_dve"], total(b, "hid_dve", 2 * e + 2))
                for t in range(2 * half, 2 * half + 2):
                    for c in range(HCH):
                        ins = pe.matmul(m[:, P * (t % 2):P * (t % 2) + P],
                                        hid[:, (HCH * e + c) % NH, P * t:P * t + P], w2s[:, e, c, :],
                                        start=(c == 0), stop=(c == HCH - 1))
                ins.then_inc(sig["down_ps"], 1)

            def ff_up(b, c):
                if b.first and c == 0:
                    pe.wait_ge(setup_dve, 3)
                for j in range(2):
                    dense(misc_bank(b, "ff_gate" if j == 0 else "ff_hid", c + 1), P,
                          wgu[:, FF1 * j + P * c:FF1 * j + P * c + P], x1T[:], "ff_ps")

            def ff_down(b):
                m = misc_bank(b, "res_b", 1)
                pe.wait_ge(sig["ff_hid"], total(b, "ff_hid"))
                for t in range(TILES):
                    for c in range(FCH):
                        ins = pe.matmul(m[:, P * t:P * t + P], hf[:, c, P * t:P * t + P], wd[:, c, :],
                                        start=(c == 0), stop=(c == FCH - 1))
                ins.then_inc(sig["ffd_ps"], 1)

            steps = dict(turn=turn, m_q=m_q, m_lat=m_lat, m_lat_turn=m_lat_turn, m_k=m_k, m_v=m_v,
                         a_q=a_q, a_k=a_k, a_v=a_v, b_q=b_q, b_k=b_k, b_v=b_v, score_max=score_max,
                         shift_turn=shift_turn, score_exp=score_exp, probs_v=probs_v, out_turn=out_turn,
                         o_turn=o_turn, o_proj=o_proj, gate=gate, up=up, down=down, ff_up=ff_up, ff_down=ff_down)
            walk(pe, steps, [turn_misc, turn_s1, turn_s2, turn_pv])

        @block.vector
        def _(v):
            turn_mx, turn_full, turn_otok, turn_factored = {}, {}, {}, {}
            v.memset(half_neg[:], -0.5).then_inc(setup_dve, 1)
            v.wait_ge(ld_w, 16 * 5)
            v.wait_ge(setup_pool, 1)

            def stats(b, src, bns, mvs, chain, done):
                for t in range(TILES):
                    ins = v.bn_stats(bns[:, t, :], src[:, t, :])
                ins.then_inc(sig[chain], 1)
                value = in_register(v, b, chain)
                v.wait_ge(setup_pool, 1)
                v.wait_ge(sig[chain], value)
                for t in range(TILES):
                    ins = v.bn_aggr(mvs[:, t, :], bns[:, t, :])
                ins.then_inc(sig[done], 1)

            def x_norm(b):
                v.wait_ge(sig["x_loaded"], total(b, "x_loaded"))
                if not b.first:
                    v.wait_ge(sig["x_rstd"], total(b.prev, "x_rstd"))
                stats(b, xs, bn[:, 0], mv[:, 0], "x_bn", "x_stats")

            def normed(dst, src, mvs, rstd, name):
                for t in range(TILES):
                    ins = v.tensor_scalar(dst[:, t, :], src[:, t, :], mvs[:, t, 0:1], rstd[:, t:t + 1],
                                          ALU.subtract, ALU.mult)
                ins.then_inc(sig[name], 1)

            def x_scaled(b):
                v.wait_ge(sig["x_rstd"], total(b, "x_rstd"))
                if not b.first:
                    v.wait_ge(sig["turned_xn"], total(b.prev, "turned_xn"))
                if not b.first:
                    v.wait_ge(sig["xr_ready"], total(b.prev, "xr_ready"))
                if not b.first:
                    v.wait_ge(sig["x2_ready"], total(b.prev, "x2_ready"))
                normed(xn, xs, mv[:, 0], sq[:, 1], "xn_ready")
                last_user(b, turn_factored, 0, "turned_xr", 1)

            def x2_scaled(b):
                last_user(b, turn_factored, 0, "turned_r2", 1)

            def x1_scaled(b):
                v.wait_ge(sig["x1_rstd"], total(b, "x1_rstd"))
                for s_last, value in last_user(b, turn_factored, 0, "turned_x1", 1):
                    v.wait_ge(s_last, value)
                normed(factored, acc, l1mv, sq1[:, 1], "x1n_ready")

            def rope_mul(b, s, first, factor):
                for s_last, value in last_user(b, turn_full, s[1], f"{s}_split", 4):
                    v.wait_ge(s_last, value)
                for j, dst in enumerate((full[s[1]], rope_s)):
                    v.wait_ge(sig[f"{s}_ps"], total(b, f"{s}_ps", j + 1))
                    if j:
                        for s_last, value in last_user(b, turn_full, "rope_s", f"{s}_full", 1):
                            v.wait_ge(s_last, value)
                    v.scalar_tensor_tensor(out=dst[:], in0=misc[SPARE["rope_dve", first + j]][:],
                                                  scalar=factor, in1=rot[:, j, :], op0=ALU.mult, op1=ALU.mult) \
                                                      .then_inc(sig["rope_dve"], 1)

            def m_q(b):
                rope_mul(b, "mq", 1, SCALE)

            def m_k(b):
                rope_mul(b, "mk", 3, 1.0)

            def m_lat(b):
                v.wait_ge(sig["lat_ps"], total(b, "lat_ps"))
                if not b.first:
                    v.wait_ge(sig["latn_ready"], total(b.prev, "latn_ready"))
                v.tensor_copy(lat[:].rearrange("p t n -> p (t n)"),
                                     misc[SPARE["lat_copied", 1]][:, 0:TILES * LATENT]).then_inc(sig["lat_copied"], 1)
                v.wait_ge(sig["lat_copied"], total(b, "lat_copied"))
                if not b.first:
                    v.wait_ge(sig["lat_rstd"], total(b.prev, "lat_rstd"))
                stats(b, lat, lbn, lmv, "lat_bn", "lat_stats")

            def m_lat_turn(b):
                v.wait_ge(sig["lat_rstd"], total(b, "lat_rstd"))
                if not b.first:
                    v.wait_ge(sig["latT_ps"], total(b.prev, "latT_ps"))
                normed(latn, lat, lmv, lsq[:, 1], "latn_ready")
                v.wait_ge(sig["latT_ps"], total(b, "latT_ps"))
                if not b.first:
                    v.wait_ge(sig["mv_ps"], total(b.prev, "mv_ps"))
                v.tensor_scalar(latT[0:LATENT, :], misc[SPARE["latT_ready", 1]][0:LATENT, :],
                                       vcol("ln_g", LATENT), vcol("ln_b", LATENT), ALU.mult, ALU.add) \
                                           .then_inc(sig["latT_ready"], 1)

            def query(b, s, ps, bias):
                v.wait_ge(sig[ps], total(b, ps, 1))
                for s_last, value in last_user(b, turn_full, s[1], f"{s}_split", 4):
                    v.wait_ge(s_last, value)
                v.tensor_scalar(full[s[1]][:], misc[SPARE[f"{s}_full", 1]][:], vcol(bias), SCALE,
                                       ALU.add, ALU.mult).then_inc(sig[f"{s}_full"], 1)

            def key(b, s, ps, bias, n):
                v.wait_ge(sig[ps], total(b, ps, 2))
                for s_last, value in last_user(b, turn_full, s[1], f"{s}_split", 4):
                    v.wait_ge(s_last, value)
                v.tensor_scalar(full[s[1]][0:n, :], misc[SPARE[f"{s}_full", 1]][0:n, :], vcol(bias, n), None,
                                       ALU.add).then_inc(sig[f"{s}_full"], 1)

            def value(b, a, ps, bias, done):
                n = kh[a]
                v.wait_ge(sig[ps], total(b, ps, 3))
                if not b.first:
                    v.wait_ge(sig[f"{a}_pv"], total(b.prev, f"{a}_pv"))
                src = misc[SPARE[done, 1]][:, 0:TILES * n * HD].rearrange("p (t h d) -> p t h d", t=TILES, d=HD)
                bv = rowv(bias).rearrange("p (h d) -> p h d", d=HD).unsqueeze(1).broadcast_to([P, TILES, n, HD])
                v.tensor_tensor(vv[a][:, :, :, 0:HD], src, bv, ALU.add).then_inc(sig[done], 1)

            def score_max(b, a, g, u):
                n = 16 * g + u
                if u == 0:
                    for s_last, value in last_user(b, turn_mx, g % 2, f"{a}_nms", 2 * g + 2):
                        v.wait_ge(s_last, value)
                if a != "M":
                    v.wait_ge(sig[f"{a}_s1_ps"], total(b, f"{a}_s1_ps", n + 1))
                    v.tensor_reduce(mx[:, g % 2, u:u + 1], s1[BANK[a, g, u]][:], AX.X, ALU.max) \
                        .then_inc(sig[f"{a}_s1_read"], 1)
                else:
                    value = in_register(v, b, "M_s1_ps", n + 1)
                    v.wait_ge(setup_pool, 1)
                    v.wait_ge(sig["M_s1_ps"], value)
                    keys, bank = P * (u % TILES + 1), s1[BANK[a, g, u]]
                    v.tensor_tensor_reduce(bank[:, 0:keys], bank[:, 0:keys], mask[:, SEQ - keys:SEQ], 1.0, LOWEST,
                                           ALU.add, ALU.max, mx[:, g % 2, u:u + 1]).then_inc(sig["M_s1_read"], 1)

            def out_turn(b, a, g):
                v.wait_ge(sig[f"{a}_ot_ps"], total(b, f"{a}_ot_ps", g + 1))
                m = misc[SPARE[f"{a}_otok", g + 1]][:].rearrange("p (t h c) -> p t h c", t=TILES, h=GROUP)
                r = rc[:, g % 2, :].rearrange("p (t h) -> p t h", t=TILES)
                v.reciprocal(r, m[:, :, :, HD]).then_inc(sig[f"{a}_rc"], 1)
                v.wait_ge(sig[f"{a}_rc"], total(b, f"{a}_rc", g + 1))
                if g == 0:
                    for s_last, value in last_user(b, turn_otok, 0, f"{a}_oT_ps", 1):
                        v.wait_ge(s_last, value)
                dst = otok[:, :, GROUP * HD * g:GROUP * HD * (g + 1)].rearrange("p t (h d) -> p t h d", h=GROUP)
                v.tensor_tensor(dst, m[:, :, :, 0:HD],
                                       r.unsqueeze(3).broadcast_to([P, TILES, GROUP, HD]), ALU.mult) \
                                           .then_inc(sig[f"{a}_otok"], 1)

            def o_proj(b, a):
                v.wait_ge(sig[f"{a}_o_ps"], total(b, f"{a}_o_ps"))
                if a == "M":
                    if not b.first:
                        v.wait_ge(sig["r2_ready"], total(b.prev, "r2_ready"))
                    if not b.first:
                        v.wait_ge(sig["acc_base"], total(b.prev, "acc_base", 1))
                    m = misc[SPARE["x2_ready", 1]][:]
                    v.tensor_tensor(x2[:], four(m), xn[:], ALU.add).then_inc(sig["x2_ready"], 1)
                if a == "A":
                    v.wait_ge(sig["acc_base"], total(b, "acc_base", 1))
                    m = misc[SPARE["gqa_added", 1]][:]
                    v.tensor_tensor(acc[:], four(m), acc[:], ALU.add).then_inc(sig["gqa_added"], 1)
                if a == "B":
                    v.wait_ge(sig["res_b"], total(b, "res_b"))
                    m = misc[SPARE["y_ready", 1]][:]
                    v.tensor_tensor(res1[:], four(m), res1[:], ALU.add).then_inc(sig["y_ready"], 1)

            def x2_norm(b):
                v.wait_ge(sig["x2_ready"], total(b, "x2_ready"))
                if not b.first:
                    v.wait_ge(sig["x2_rstd"], total(b.prev, "x2_rstd"))
                stats(b, x2, bn[:, 1], mv[:, 1], "x2_bn", "x2_stats")

            def gate(b):
                if b.first:
                    v.wait_ge(ld_int, 16 * 2)
                    v.tensor_scalar(wgu[:], wi[:, 0:2 * FF1], 1.0 / 127.0, None, ALU.mult).then_inc(setup_dve, 1)
                    v.tensor_scalar(wd[:].rearrange("p c d -> p (c d)"), wi[:, 2 * FF1:3 * FF1], 1.0 / 127.0, 0.5,
                                    ALU.mult, ALU.mult).then_inc(setup_dve, 1)
                v.wait_ge(sig["gate_ps"], total(b, "gate_ps"))
                if not b.first:
                    v.wait_ge(sig["one_hot"], total(b.prev, "one_hot"))
                m = misc[SPARE["logits", 1]][:, 0:TILES * EXPERTS].rearrange("p (t e) -> p t e", t=TILES)
                v.tensor_tensor(lg[:], m, rowv("gate_b").unsqueeze(1).broadcast_to([P, TILES, EXPERTS]),
                                       ALU.add).then_inc(sig["logits"], 1)
                v.wait_ge(sig["logits"], total(b, "logits"))
                v.tensor_reduce(lmax[:], lg[:], AX.X, ALU.max).then_inc(sig["top"], 1)
                v.wait_ge(sig["top"], total(b, "top"))
                v.tensor_tensor(eq[:], lg[:], spread(lmax[:], EXPERTS), ALU.is_equal).then_inc(sig["ties"], 1)

            def up(b, e, c):
                n = HCH * e + c
                if n % 2:
                    return
                if b.first and n == 0:
                    v.wait_ge(setup_dve, 3)
                v.wait_ge(sig["up_ps"], total(b, "up_ps", n + 1))
                if not b.first or e > 1:
                    v.wait_ge(sig["down_ps"], total(b, "down_ps", 2 * e - 2))
                v.tensor_scalar(hid[:, n % NH, :], misc[SPARE["hid_dve", n // 2 + 1]][:],
                                       vcol("b1", k=n), 0.0, ALU.add, ALU.max).then_inc(sig["hid_dve"], 1)

            def down(b, e, half):
                n = 2 * e + half
                v.wait_ge(sig["down_ps"], total(b, "down_ps", n + 1))
                v.wait_ge(sig["acc_base"], total(b, "acc_base"))
                if not b.first or n > 1:
                    v.wait_ge(sig["acc_dve"], total(b, "acc_dve", n - 1))
                m = misc[SPARE["acc_dve", n + 1]]
                for j in range(2):
                    t = 2 * half + j
                    ins = v.scalar_tensor_tensor(out=acc[:, t, :], in0=m[:, P * j:P * j + P],
                                                 scalar=oneh[:, t, e:e + 1], in1=acc[:, t, :],
                                                 op0=ALU.mult, op1=ALU.add)
                ins.then_inc(sig["acc_dve"], 1)

            def x1_norm(b):
                v.wait_ge(sig["acc_dve"], total(b, "acc_dve"))
                if not b.first:
                    v.wait_ge(sig["x1_rstd"], total(b.prev, "x1_rstd"))
                stats(b, acc, l1bn, l1mv, "x1_bn", "x1_stats")

            def ff_up(b, c):
                v.wait_ge(sig["tanh_done"], total(b, "tanh_done", c + 1))
                v.scalar_tensor_tensor(out=th[:], in0=th[:], scalar=1.0, in1=misc[SPARE["ff_gate", c + 1]][:],
                                              op0=ALU.add, op1=ALU.mult).then_inc(sig["ff_gate"], 1)
                v.wait_ge(sig["ff_gate"], total(b, "ff_gate", c + 1))
                v.wait_ge(sig["ff_ps"], total(b, "ff_ps", 2 * c + 2))
                if not b.first:
                    v.wait_ge(sig["ffd_ps"], total(b.prev, "ffd_ps"))
                v.tensor_tensor(hf[:, c, :], th[:], misc[SPARE["ff_hid", c + 1]][:], ALU.mult) \
                    .then_inc(sig["ff_hid"], 1)

            def ff_down(b):
                v.wait_ge(sig["ffd_ps"], total(b, "ffd_ps"))
                v.wait_ge(sig["res1_ready"], total(b, "res1_ready"))
                v.tensor_tensor(res1[:], four(misc[SPARE["res_b", 1]][:]), res1[:], ALU.add).then_inc(sig["res_b"], 1)

            steps = dict(x_norm=x_norm, x_scaled=x_scaled, x1_scaled=x1_scaled, x2_scaled=x2_scaled,
                         m_q=m_q, m_k=m_k, m_lat=m_lat,
                         m_lat_turn=m_lat_turn,
                         a_q=lambda b: query(b, "aq", "a_ps", "a_bq"),
                         a_k=lambda b: key(b, "ak", "a_ps", "a_bk", KV0 * HD),
                         a_v=lambda b: value(b, "A", "a_ps", "a_bv", "av_ready"),
                         b_q=lambda b: query(b, "bq", "b_ps", "b_bq"),
                         b_k=lambda b: key(b, "bk", "b_ps", "b_bk", HD),
                         b_v=lambda b: value(b, "B", "b_ps", "b_bv", "bv_ready"),
                         score_max=score_max, out_turn=out_turn, o_proj=o_proj,
                         x2_norm=x2_norm, gate=gate, up=up, down=down,
                         x1_norm=x1_norm, ff_up=ff_up, ff_down=ff_down)
            walk(v, steps, [turn_mx, turn_full, turn_otok, turn_factored],
                 ordered({"o_proj": 0.024}))

        @block.scalar
        def _(act):
            turn_probs, turn_osb, turn_oT, turn_nmT, turn_factored = {}, {}, {}, {}, {}
            act.wait_ge(ld_w, 16 * 5)
            act.wait_ge(setup_pool, 1)

            def turn(b, what):
                dst = {"xn": xnT, "x1": x1T, "xr": xrT, "r2": r2T}[what]
                act.wait_ge(sig["turned_" + what], total(b, "turned_" + what))
                for reader in {"xn": ("a_ps",), "x1": ("b_ps", "ff_ps"),
                               "xr": ("mq_ps", "lat_ps"), "r2": ("up_ps",)}[what]:
                    if not b.first:
                        act.wait_ge(sig[reader], total(b.prev, reader))
                src = misc[SPARE[what + "_T", 1]][:]
                if what in ("xr", "r2"):
                    ins = act.activation(dst[:], src, ACT.Identity, scale=vcol("norm1" if what == "xr" else "norm2"))
                else:
                    ins = act.activation(dst[:], src, ACT.Copy)
                ins.then_inc(sig[what + "_T"], 1)

            def scaled(src, factor, name):
                for t in range(TILES):
                    ins = act.activation(factored[:, t, :], src[:, t, :], ACT.Copy, scale=factor[:, t:t + 1])
                ins.then_inc(sig[name], 1)

            def x_scaled(b):
                act.wait_ge(sig["xn_ready"], total(b, "xn_ready"))
                for s_last, value in last_user(b, turn_factored, 0, "turned_xr", 1):
                    act.wait_ge(s_last, value)
                scaled(xn, sq[:, 6], "xr_ready")

            def x2_scaled(b):
                act.wait_ge(sig["x2_rstd"], total(b, "x2_rstd"))
                for s_last, value in last_user(b, turn_factored, 0, "turned_r2", 1):
                    act.wait_ge(s_last, value)
                scaled(x2, sq2[:, 3], "r2_ready")

            def x1_scaled(b):
                last_user(b, turn_factored, 0, "turned_x1", 1)

            def m_v(b):
                act.wait_ge(sig["mv_ps"], total(b, "mv_ps"))
                if not b.first:
                    act.wait_ge(sig["M_pv"], total(b.prev, "M_pv"))
                dst = vv["M"][:].rearrange("p t h c -> p (t h) c")[:, :, 0:HD]
                act.activation(dst, misc[SPARE["mv_ready", 1]][:].rearrange("p (n d) -> p n d", d=HD),
                                      ACT.Copy).then_inc(sig["mv_ready"], 1)

            def shift_turn(b, a, g):
                for s_last, value in last_user(b, turn_nmT, g % 2, f"{a}_shift", 32 * (g + 1)):
                    act.wait_ge(s_last, value)
                act.wait_ge(sig[f"{a}_nmT_ps"], total(b, f"{a}_nmT_ps", g + 1))
                act.activation(nmT[:, g % 2, :], misc[SPARE[f"{a}_nmT", g + 1]][:].bitcast(BF16)[0:32, 0:P],
                               ACT.Copy).then_inc(sig[f"{a}_nmT"], 1)

            def score_exp(b, a, g, u):
                n = UNITS2[a] * g + u
                act.wait_ge(sig[f"{a}_s2_ps"], total(b, f"{a}_s2_ps", n + 1))
                slot = SLOT[a, g, u]
                for s_last, value in last_user(b, turn_probs, slot, f"{a}_pv", n + 1):
                    act.wait_ge(s_last, value)
                act.activation(probs[:, slot, :], s2[n % 2][:], ACT.Exp).then_inc(sig[f"{a}_exp"], 1)

            def out_copy(b, a, g):
                act.wait_ge(sig[f"{a}_pv"], total(b, f"{a}_pv", UNITS2[a] * (g + 1)))
                for s_last, value in last_user(b, turn_osb, g % 2, f"{a}_ot_ps", g + 1):
                    act.wait_ge(s_last, value)
                act.activation(osb[:, g % 2, :], pv[g % NPV][:], ACT.Copy).then_inc(sig[f"{a}_osb"], 1)

            def o_turn(b, a):
                act.wait_ge(sig[f"{a}_oT_ps"], total(b, f"{a}_oT_ps"))
                for s_last, value in last_user(b, turn_oT, 0, f"{a}_o_ps", 1):
                    act.wait_ge(s_last, value)
                act.activation(oT[:], misc[SPARE[f"{a}_oT", 1]][:], ACT.Copy).then_inc(sig[f"{a}_oT"], 1)

            def up(b, e, c):
                n = HCH * e + c
                if n % 2 == 0:
                    return
                if b.first and n == 1:
                    act.wait_ge(setup_dve, 3)
                act.wait_ge(sig["up_ps"], total(b, "up_ps", n + 1))
                if not b.first or e > 1:
                    act.wait_ge(sig["down_ps"], total(b, "down_ps", 2 * e - 2))
                act.activation(hid[:, n % NH, :], misc[SPARE["hid_act", n // 2 + 1]][:], ACT.Relu,
                                      bias=vcol("b1", k=n)).then_inc(sig["hid_act"], 1)

            def ff_up(b, c):
                act.wait_ge(sig["ff_ps"], total(b, "ff_ps", 2 * c + 1))
                if not b.first or c:
                    act.wait_ge(sig["ff_hid"], total(b, "ff_hid", c))
                act.activation(th[:], misc[SPARE["ff_gate", c + 1]][:], ACT.Tanh, scale=0.5) \
                    .then_inc(sig["tanh_done"], 1)

            walk(act, dict(turn=turn, x_scaled=x_scaled, x2_scaled=x2_scaled, x1_scaled=x1_scaled,
                           m_v=m_v, shift_turn=shift_turn,
                           score_exp=score_exp, out_copy=out_copy, o_turn=o_turn, up=up,
                           ff_up=ff_up), [turn_probs, turn_osb, turn_oT, turn_nmT, turn_factored])

        @block.gpsimd
        def _(pool):
            turn_nms, turn_parts = {}, {}
            done = [0]

            def link(ins):
                done[0] += 1
                ins.then_inc(pool_chain, 1)
                pool.wait_ge(pool_chain, done[0])

            for m in (ident, identb):
                link(pool.memset(m[:], 0.0))
                link(pool.affine_select(out=m[:], in_=m[:], compare_op=ALU.not_equal, fill=1.0, base=0,
                                        pattern=[[-1, P]], channel_multiplier=1))
            link(pool.memset(mask[:], 0.0))
            link(pool.affine_select(out=mask[:, SEQ - P:SEQ], in_=mask[:, SEQ - P:SEQ], compare_op=ALU.is_ge,
                                    fill=MASKED, base=0, pattern=[[-1, P]], channel_multiplier=1))
            link(pool.memset(latT[:], 0.0))
            link(pool.memset(minus[:], -1.0))
            for a in "MBA":
                link(pool.memset(vv[a][:], 0.0))
                link(pool.memset(vv[a][:, :, :, HD:HD + 1], 1.0))
            pool.wait_ge(setup_dve, 1)
            pool.wait_ge(ld_w, 16 * 5)
            pool.memset(seen[:], 0.0).then_inc(setup_pool, 1)

            def chain(b, name, k, ins):
                ins.then_inc(sig[name], 1)
                value = in_register(pool, b, name, k)
                pool.wait_ge(setup_pool, 1)
                pool.wait_ge(sig[name], value)

            def power(dst, src):
                return pool.tensor_tensor(dst, src, half_neg[:], ALU.pow)

            def x_norm(b):
                value = in_register(pool, b, "x_stats")
                pool.wait_ge(setup_pool, 1)
                pool.wait_ge(sig["x_stats"], value)
                if not b.first:
                    value = in_register(pool, b.prev, "xr_ready")
                    pool.wait_ge(setup_pool, 1)
                    pool.wait_ge(sig["xr_ready"], value)
                var = mv[:, 0, :, 1]
                chain(b, "x_rstd", 1, pool.tensor_scalar(sq[:, 0, :], var, 1.0, 1e-5, ALU.mult, ALU.add))
                chain(b, "x_rstd", 2, power(sq[:, 1, :], sq[:, 0, :]))
                chain(b, "x_rstd", 3, pool.tensor_tensor(sq[:, 2, :], var, sq[:, 1, :], ALU.mult))
                chain(b, "x_rstd", 4, pool.tensor_tensor(sq[:, 3, :], sq[:, 2, :], sq[:, 1, :], ALU.mult))
                chain(b, "x_rstd", 5, pool.tensor_scalar(sq[:, 4, :], sq[:, 3, :], 1.0, 1e-6, ALU.mult, ALU.add))
                chain(b, "x_rstd", 6, power(sq[:, 5, :], sq[:, 4, :]))
                pool.tensor_scalar(sq[:, 6, :], sq[:, 5, :], 1.0, 0.0, ALU.mult, ALU.add).then_inc(sig["x_rstd"], 1)
                if not b.first:
                    value = in_register(pool, b.prev, "acc_base", 1)
                    pool.wait_ge(setup_pool, 1)
                    pool.wait_ge(sig["acc_base"], value)
                pool.tensor_tensor(res0[:], xs[:], rowv("a_bo").unsqueeze(1).broadcast_to([P, TILES, D]),
                                          ALU.add).then_inc(sig["res0_ready"], 1)

            def m_lat(b):
                value = in_register(pool, b, "lat_stats")
                pool.wait_ge(setup_pool, 1)
                pool.wait_ge(sig["lat_stats"], value)
                if not b.first:
                    value = in_register(pool, b.prev, "latn_ready")
                    pool.wait_ge(setup_pool, 1)
                    pool.wait_ge(sig["latn_ready"], value)
                chain(b, "lat_rstd", 1, pool.tensor_scalar(lsq[:, 0, :], lmv[:, :, 1], 1.0, 1e-5, ALU.mult, ALU.add))
                power(lsq[:, 1, :], lsq[:, 0, :]).then_inc(sig["lat_rstd"], 1)

            def rotated(b, s, k):
                value = in_register(pool, b, "rope_dve", k)
                pool.wait_ge(setup_pool, 1)
                pool.wait_ge(sig["rope_dve"], value)
                f = full[s[1]]
                pool.tensor_tensor(f[:], f[:], rope_s[:], ALU.add).then_inc(sig[f"{s}_full"], 1)

            def split(b, s):
                n = P if s[1] == "q" else kh[s[0].upper()] * HD
                f, r, p = full[s[1]][0:n, :], rest[0:n, :], parts[s[1]]
                value = in_register(pool, b, f"{s}_full")
                pool.wait_ge(setup_pool, 1)
                pool.wait_ge(sig[f"{s}_full"], value)
                for s_last, value in last_user(b, turn_parts, s[1], f"{s}_stored", 16, pool):
                    pool.wait_ge(setup_pool, 1)
                    pool.wait_ge(s_last, value)
                chain(b, f"{s}_split", 1, pool.tensor_scalar(p[0:n, 0, :], f, 1.0, 0.0, ALU.mult, ALU.add))
                chain(b, f"{s}_split", 2, pool.tensor_tensor(r, f, p[0:n, 0, :], ALU.subtract))
                chain(b, f"{s}_split", 3, pool.tensor_scalar(p[0:n, 1, :], r, 1.0, 0.0, ALU.mult, ALU.add))
                chain(b, f"{s}_split", 4, pool.tensor_tensor(p[0:n, 2, :], r, p[0:n, 1, :], ALU.subtract))

            def shift_split(b, a, g):
                value = in_register(pool, b, f"{a}_s1_read", 16 * (g + 1))
                pool.wait_ge(setup_pool, 1)
                pool.wait_ge(sig[f"{a}_s1_read"], value)
                for s_last, value in last_user(b, turn_nms, g % 2, f"{a}_nmT_ps", g + 1, pool):
                    pool.wait_ge(setup_pool, 1)
                    pool.wait_ge(s_last, value)
                chain(b, f"{a}_nms", 2 * g + 1,
                      pool.tensor_scalar(nms[:, g % 2, 0, :], mx[:, g % 2, :], 1.0, 0.0, ALU.mult, ALU.add))
                pool.tensor_tensor(nms[:, g % 2, 1, :], mx[:, g % 2, :], nms[:, g % 2, 0, :], ALU.subtract) \
                    .then_inc(sig[f"{a}_nms"], 1)

            def score_exp(b, a, g, u):
                if a != "M":
                    return
                n = UNITS2[a] * g + u
                value = in_register(pool, b, "M_exp", n + 1)
                pool.wait_ge(setup_pool, 1)
                pool.wait_ge(sig["M_exp"], value)
                p = probs[:, SLOT[a, g, u], :]
                r = u % 5
                if r in (0, 2):
                    v, pattern = p[:, 0:P], [[1, P]]
                elif r in (1, 3):
                    v, pattern = p.rearrange("p (n q) -> p n q", q=P)[:, 0:4:3, :], [[0, 2], [1, P]]
                else:
                    v, pattern = p.rearrange("p (n q) -> p n q", q=P)[:, 0:4:2, :], [[0, 2], [1, P]]
                pool.affine_select(out=v, in_=v, compare_op=ALU.is_ge, fill=0.0, base=0, pattern=pattern,
                                          channel_multiplier=-1).then_inc(sig["M_masked"], 1)

            def x2_norm(b):
                value = in_register(pool, b, "x2_ready")
                pool.wait_ge(setup_pool, 1)
                pool.wait_ge(sig["x2_ready"], value)
                value = in_register(pool, b, "res0_ready")
                pool.wait_ge(setup_pool, 1)
                pool.wait_ge(sig["res0_ready"], value)
                if not b.first:
                    value = in_register(pool, b.prev, "x1n_ready")
                    pool.wait_ge(setup_pool, 1)
                    pool.wait_ge(sig["x1n_ready"], value)
                pool.tensor_tensor(acc[:], x2[:], res0[:], ALU.add).then_inc(sig["acc_base"], 1)
                value = in_register(pool, b, "x2_stats")
                pool.wait_ge(setup_pool, 1)
                pool.wait_ge(sig["x2_stats"], value)
                if not b.first:
                    value = in_register(pool, b.prev, "r2_ready")
                    pool.wait_ge(setup_pool, 1)
                    pool.wait_ge(sig["r2_ready"], value)
                mean, var = mv[:, 1, :, 0], mv[:, 1, :, 1]
                chain(b, "x2_rstd", 1, pool.tensor_tensor(sq2[:, 0, :], mean, mean, ALU.mult))
                chain(b, "x2_rstd", 2, pool.tensor_tensor(sq2[:, 1, :], sq2[:, 0, :], var, ALU.add))
                chain(b, "x2_rstd", 3, pool.tensor_scalar(sq2[:, 2, :], sq2[:, 1, :], 1.0, 1e-6, ALU.mult, ALU.add))
                power(sq2[:, 3, :], sq2[:, 2, :]).then_inc(sig["x2_rstd"], 1)

            def gate(b):
                value = in_register(pool, b, "ties")
                pool.wait_ge(setup_pool, 1)
                pool.wait_ge(sig["ties"], value)
                if not b.first:
                    value = in_register(pool, b.prev, "acc_dve")
                    pool.wait_ge(setup_pool, 1)
                    pool.wait_ge(sig["acc_dve"], value)
                e = [eq[:, :, n] for n in range(EXPERTS)]
                o = [oneh[:, :, n] for n in range(EXPERTS)]
                chain(b, "one_hot", 1, pool.tensor_scalar(o[0], e[0], 1.0, 0.0, ALU.mult, ALU.add))
                chain(b, "one_hot", 2, pool.tensor_scalar(seen[:, 0, :], e[0], -1.0, 1.0, ALU.mult, ALU.add))
                chain(b, "one_hot", 3, pool.tensor_tensor(o[1], e[1], seen[:, 0, :], ALU.mult))
                chain(b, "one_hot", 4, pool.tensor_tensor(seen[:, 1, :], seen[:, 0, :], o[1], ALU.subtract))
                chain(b, "one_hot", 5, pool.tensor_tensor(o[2], e[2], seen[:, 1, :], ALU.mult))
                chain(b, "one_hot", 6, pool.tensor_tensor(seen[:, 0, :], seen[:, 1, :], o[2], ALU.subtract))
                chain(b, "one_hot", 7, pool.tensor_tensor(o[3], e[3], seen[:, 0, :], ALU.mult))

            def add_b2(b, n):
                if n == 0:
                    value = in_register(pool, b, "gqa_added")
                    pool.wait_ge(setup_pool, 1)
                    pool.wait_ge(sig["gqa_added"], value)
                picked = four(rest[:])
                b2 = rowv("b2")[:, D * n:D * n + D].unsqueeze(1).broadcast_to([P, TILES, D])
                chain(b, "b2_term", n + 1, pool.tensor_tensor(picked, b2, spread(oneh[:, :, n], D), ALU.mult))
                chain(b, "acc_base", n + 2, pool.tensor_tensor(acc[:], acc[:], picked, ALU.add))

            def x1_norm(b):
                value = in_register(pool, b, "x1_stats")
                pool.wait_ge(setup_pool, 1)
                pool.wait_ge(sig["x1_stats"], value)
                if not b.first:
                    value = in_register(pool, b.prev, "x1n_ready")
                    pool.wait_ge(setup_pool, 1)
                    pool.wait_ge(sig["x1n_ready"], value)
                chain(b, "x1_rstd", 1, pool.tensor_scalar(sq1[:, 0, :], l1mv[:, :, 1], 1.0, 1e-5, ALU.mult, ALU.add))
                power(sq1[:, 1, :], sq1[:, 0, :]).then_inc(sig["x1_rstd"], 1)
                if not b.first:
                    value = in_register(pool, b.prev, "y_stored")
                    pool.wait_ge(setup_pool, 1)
                    pool.wait_ge(sig["y_stored"], value)
                pool.tensor_tensor(res1[:], acc[:], rowv("b_bo").unsqueeze(1).broadcast_to([P, TILES, D]),
                                          ALU.add).then_inc(sig["res1_ready"], 1)

            walk(pool, dict(x_norm=x_norm, m_lat=m_lat, m_q=lambda b: rotated(b, "mq", 2),
                            m_k=lambda b: rotated(b, "mk", 4), split=split, shift_split=shift_split,
                            score_exp=score_exp, x2_norm=x2_norm, gate=gate, add_b2=add_b2,
                            x1_norm=x1_norm), [turn_nms, turn_parts],
                 ordered({"x_norm": 0.1, "x1_norm": 0.15, "x2_norm": 0.042, "m_lat": 0.1, "gate": 0.1,
                          "m_q": 0.05, "m_k": 0.05}))


def kernel(**inputs):
    import concourse.bacc as bacc
    from concourse.bass_utils import run_bass_kernel_spmd

    a = {n: np.asarray(v) for n, v in inputs.items()}
    swap = np.arange(D) ^ (HD // 2)

    def attn(n):
        return a["L0_attn_" + n]

    def ffn(n):
        return a["L0_ffn_" + n]

    def l1(n):
        return a["L1_attn_" + n]

    cols = {"a_wq": attn("wq").T, "a_wk": attn("wk").T, "a_wv": attn("wv").T,
            "a_wo": attn("wo").T,
            "m_wq": ffn("Wq").T, "m_wqs": ffn("Wq").T[:, swap], "m_wdkv": ffn("Wdkv").T, "m_wo": ffn("Wo").T,
            "gate": ffn("gate_w").T, "b_wq": l1("Wq"), "b_wk": l1("Wk"), "b_wv": l1("Wv"), "b_wo": l1("Wo")}
    w_all = np.concatenate([cols[n] for n in WCOLS], axis=1)
    w_lat = np.zeros((P, 384), np.float32)
    w_lat[:LATENT] = np.concatenate([ffn("Wuk").T, ffn("Wuk").T[:, swap], ffn("Wuv").T], axis=1)
    v_all = np.zeros((P, VN), np.float32)
    for n, src in (("a_bq", attn("bq")), ("a_bk", attn("bk")), ("norm1", ffn("norm1_w")), ("norm2", ffn("norm2_w")),
                   ("ln_g", ffn("ln_g")), ("ln_b", ffn("ln_b")), ("b_bq", l1("bq")), ("b_bk", l1("bk"))):
        v_all[:len(src), VCOLS[n]] = src
    v_all[:, VCOLS["b1"]:] = ffn("b1").reshape(EXPERTS * HCH, P).T
    rows = {"a_bv": attn("bv"), "a_bo": attn("bo"), "gate_b": ffn("gate_b"), "b2": ffn("b2").reshape(-1),
            "b_bv": l1("bv"), "b_bo": l1("bo")}
    r_all = np.concatenate([rows[n] for n in RCOLS])
    w1 = ffn("W1").transpose(2, 0, 1).reshape(D, EXPERTS * HIDDEN)
    w2 = ffn("W2").transpose(2, 0, 1).reshape(HCH, P, EXPERTS, D).transpose(1, 2, 0, 3)
    wi_up = np.concatenate([a["L1_ffn_w_gate"].T, a["L1_ffn_w_up"].T], axis=1)
    wi_down = a["L1_ffn_w_down"].T.reshape(FCH, P, D).transpose(1, 0, 2).reshape(P, FF1)

    half = HD // 2
    inv_freq = (1.0 / 10000.0 ** (np.arange(half, dtype=np.float32) / half)).astype(np.float32)
    angle = np.arange(SEQ, dtype=np.float32)[:, None] * inv_freq[None, :]
    ch = np.arange(D) % HD
    cos, sin = np.cos(angle).T[ch % half], np.sin(angle).T[ch % half]
    sin = sin * np.where(ch < half, -1.0, 1.0)[:, None]
    rope = np.stack([cos, sin], axis=1).astype(np.float32)

    nc = bacc.Bacc("TRN2", target_bir_lowering=False, num_devices=1)
    arrays, args = {}, []
    for name, arr in (("x", attn("x")), ("w_all", w_all), ("w_lat", w_lat), ("v_all", v_all), ("r_all", r_all),
                      ("w1", w1), ("w2", w2), ("wi_up", wi_up), ("wi_down", wi_down), ("rope", rope)):
        arr = np.ascontiguousarray(arr)
        arrays[name] = arr
        args.append(nc.dram_tensor(name, arr.shape, mybir.dt.from_np(arr.dtype), kind="ExternalInput").ap())
    args.append(nc.dram_tensor("out", (BATCH, SEQ, D), F32, kind="ExternalOutput").ap())
    kernel_program(nc, *args)
    r = run_bass_kernel_spmd(nc, [arrays], core_ids=[0])
    return r.results[0]["out"]
```
